# Optimizing a Trainium2 kernel written in Bass

```python
import numpy as np
import jax
import jax.numpy as jnp

def _softmax(x, axis=-1):
    return jax.nn.softmax(x, axis=axis)

def _gelu(x):
    return jax.nn.gelu(x, approximate=True)

def _silu(x):
    return jax.nn.silu(x)

def _sigmoid(x):
    return jax.nn.sigmoid(x)

def _layernorm(x, axis=-1, eps=1e-05):
    m = jnp.mean(x, axis=axis, keepdims=True)
    v = jnp.var(x, axis=axis, keepdims=True)
    return (x - m) / jnp.sqrt(v + eps)

def _scatter_add(tgt, idx, src, axis=0):
    return tgt.at[idx].add(src)

def _segment_sum(src, seg, n):
    return jax.ops.segment_sum(src, seg, n)
kernel_name = 'mk_seq_postln_d1_jaxref_r4_b0db05'

def setup_inputs(seed: int=0):
    np.random.seed(seed)
    _w = jnp.asarray

    def _L0_attn_setup():
        import jax, jax.numpy as jnp
        import numpy as np
        NUM_HEADS = 16
        ROPE_THETA = 10000.0

        def _rope_cos_sin(head_dim, seq_len, theta=ROPE_THETA):
            exps = -jnp.arange(0, head_dim, 2)[:head_dim // 2].astype(jnp.float32) / head_dim
            freqs = theta ** exps
            ang = jnp.arange(seq_len, dtype=jnp.float32)[:, None] * freqs[None, :]
            return (jnp.cos(ang), jnp.sin(ang))

        def _apply_rope(x, cos, sin):
            x2 = x.reshape(*x.shape[:-1], -1, 2)
            xr, xi = (x2[..., 0], x2[..., 1])
            c = cos[None, None]
            s = sin[None, None]
            outr = xr * c - xi * s
            outi = xr * s + xi * c
            return jnp.stack([outr, outi], axis=-1).reshape(x.shape)
        key = jax.random.key(seed)
        ks = jax.random.split(key, 9)
        B, S, D = (2, 512, 256)
        scale = 0.02
        x = jax.random.normal(ks[0], (B, S, D), jnp.float32)
        Wq = jax.random.normal(ks[1], (D, D), jnp.float32) * scale
        bq = jax.random.normal(ks[2], (D,), jnp.float32) * scale
        Wk = jax.random.normal(ks[3], (D, D), jnp.float32) * scale
        bk = jax.random.normal(ks[4], (D,), jnp.float32) * scale
        Wv = jax.random.normal(ks[5], (D, D), jnp.float32) * scale
        bv = jax.random.normal(ks[6], (D,), jnp.float32) * scale
        Wo = jax.random.normal(ks[7], (D, D), jnp.float32) * scale
        return {'x': x, 'Wq': Wq, 'bq': bq, 'Wk': Wk, 'bk': bk, 'Wv': Wv, 'bv': bv, 'Wo': Wo}
    _L0_attn_in = _L0_attn_setup()

    def _L0_ffn_setup():
        import jax, jax.numpy as jnp
        import numpy as np
        DIM = 256
        DEPTH = 2
        HEADS = 8
        DIM_HEAD = 64
        WINDOW = 128
        INNER = HEADS * DIM_HEAD
        HID = int(DIM * 4 * 2 / 3)
        B, N = (2, 2048)
        QK_SCALE = 8.0

        def shift_token(t):
            t1, t2 = jnp.split(t, 2, axis=-1)
            t2 = jnp.pad(t2, ((0, 0), (1, 0), (0, 0)))[:, :-1]
            return jnp.concatenate([t1, t2], axis=-1)

        def l2norm(t):
            return t / jnp.clip(jnp.linalg.norm(t, axis=-1, keepdims=True), 1e-12)

        def rotate_half(x):
            x1, x2 = jnp.split(x, 2, axis=-1)
            return jnp.concatenate([-x2, x1], axis=-1)

        def rotary_xpos(q, k):
            n = q.shape[-2]
            half_idx = jnp.arange(0, DIM_HEAD, 2, dtype=jnp.float32)
            inv_freq = 1.0 / 10000.0 ** (half_idx / DIM_HEAD)
            t = jnp.arange(n, dtype=jnp.float32)
            freqs = t[:, None] * inv_freq[None, :]
            freqs = jnp.concatenate([freqs, freqs], axis=-1)
            base = (half_idx + 0.4 * DIM_HEAD) / (1.4 * DIM_HEAD)
            power = (t - n // 2) / float(WINDOW // 2)
            scale = base[None, :] ** power[:, None]
            scale = jnp.concatenate([scale, scale], axis=-1)
            cos, sin = (jnp.cos(freqs), jnp.sin(freqs))
            q = q * cos * scale + rotate_half(q) * sin * scale
            k = k * cos / scale + rotate_half(k) * sin / scale
            return (q, k)

        def local_attention(q, k, v):
            b, h, n, d = q.shape
            w = n // WINDOW
            bq = q.reshape(b, h, w, WINDOW, d) * QK_SCALE
            bk = k.reshape(b, h, w, WINDOW, d)
            bv = v.reshape(b, h, w, WINDOW, d)

            def look_around(t):
                p = jnp.pad(t, ((0, 0), (0, 0), (1, 0), (0, 0), (0, 0)))
                return jnp.concatenate([p[:, :, :w], p[:, :, 1:]], axis=3)
            bk, bv = (look_around(bk), look_around(bv))
            bt = jnp.arange(n).reshape(w, WINDOW)
            btp = jnp.pad(bt, ((1, 0), (0, 0)), constant_values=-1)
            btk = jnp.concatenate([btp[:w], btp[1:]], axis=1)
            sim = jnp.einsum('bhwid,bhwjd->bhwij', bq, bk)
            i = bt[:, :, None]
            j = btk[:, None, :]
            mask = (i < j) | (i > j + WINDOW) | (j == -1)
            sim = jnp.where(mask, -jnp.finfo(sim.dtype).max, sim)
            attn = jax.nn.softmax(sim, axis=-1)
            out = jnp.einsum('bhwij,bhwjd->bhwid', attn, bv)
            return out.reshape(b, h, n, d)

        def _layer(x, wqkv, qs, ksc, wo, lg, lb, w1, b1, w2, b2):
            b, n, _ = x.shape
            h = shift_token(x)
            qkv = h @ wqkv
            q, k, v = jnp.split(qkv, 3, axis=-1)
            to_heads = lambda t: t.reshape(b, n, HEADS, DIM_HEAD).transpose(0, 2, 1, 3)
            q, k, v = (to_heads(q), to_heads(k), to_heads(v))
            q = l2norm(q) * qs
            k = l2norm(k) * ksc
            q, k = rotary_xpos(q, k)
            o = local_attention(q, k, v)
            o = o.transpose(0, 2, 1, 3).reshape(b, n, INNER)
            x = x + o @ wo
            h = shift_token(x)
            mu = h.mean(-1, keepdims=True)
            var = h.var(-1, keepdims=True)
            h = (h - mu) / jnp.sqrt(var + 1e-05) * lg + lb
            h = h @ w1 + b1
            a, g = jnp.split(h, 2, axis=-1)
            h = a * jax.nn.gelu(g, approximate=False)
            x = x + h @ w2 + b2
            return x
        key = jax.random.key(seed)
        ks = jax.random.split(key, 6)
        return {'x': jax.random.normal(ks[0], (B, N, DIM), jnp.float32), 'wqkv': jax.random.normal(ks[1], (DEPTH, DIM, 3 * INNER), jnp.float32) * 0.02, 'q_scale': jnp.ones((DEPTH, DIM_HEAD), jnp.float32), 'k_scale': jnp.ones((DEPTH, DIM_HEAD), jnp.float32), 'wo': jax.random.normal(ks[2], (DEPTH, INNER, DIM), jnp.float32) * 0.02, 'ln_g': jnp.ones((DEPTH, DIM), jnp.float32), 'ln_b': jnp.zeros((DEPTH, DIM), jnp.float32), 'w1': jax.random.normal(ks[3], (DEPTH, DIM, 2 * HID), jnp.float32) * 0.02, 'b1': jnp.zeros((DEPTH, 2 * HID), jnp.float32), 'w2': jax.random.normal(ks[4], (DEPTH, HID, DIM), jnp.float32) * 0.02, 'b2': jnp.zeros((DEPTH, DIM), jnp.float32)}
    _L0_ffn_in = _L0_ffn_setup()
    _d = {'L0_attn_x': _L0_attn_in['x'], 'L0_attn_Wq': _L0_attn_in['Wq'], 'L0_attn_bq': _L0_attn_in['bq'], 'L0_attn_Wk': _L0_attn_in['Wk'], 'L0_attn_bk': _L0_attn_in['bk'], 'L0_attn_Wv': _L0_attn_in['Wv'], 'L0_attn_bv': _L0_attn_in['bv'], 'L0_attn_Wo': _L0_attn_in['Wo'], 'L0_ffn_wqkv': _L0_ffn_in['wqkv'], 'L0_ffn_q_scale': _L0_ffn_in['q_scale'], 'L0_ffn_k_scale': _L0_ffn_in['k_scale'], 'L0_ffn_wo': _L0_ffn_in['wo'], 'L0_ffn_ln_g': _L0_ffn_in['ln_g'], 'L0_ffn_ln_b': _L0_ffn_in['ln_b'], 'L0_ffn_w1': _L0_ffn_in['w1'], 'L0_ffn_b1': _L0_ffn_in['b1'], 'L0_ffn_w2': _L0_ffn_in['w2'], 'L0_ffn_b2': _L0_ffn_in['b2']}
    _x0 = _d['L0_attn_x']
    _d['L0_attn_x'] = jax.random.normal(jax.random.fold_in(jax.random.key(seed), 1), (8, 1024, 256), dtype=_x0.dtype)
    del _x0
    return _d

def reference(L0_attn_x, L0_attn_Wq, L0_attn_bq, L0_attn_Wk, L0_attn_bk, L0_attn_Wv, L0_attn_bv, L0_attn_Wo, L0_ffn_wqkv, L0_ffn_q_scale, L0_ffn_k_scale, L0_ffn_wo, L0_ffn_ln_g, L0_ffn_ln_b, L0_ffn_w1, L0_ffn_b1, L0_ffn_w2, L0_ffn_b2):

    def _L0_attn_ref(x, Wq, bq, Wk, bk, Wv, bv, Wo):
        import jax, jax.numpy as jnp
        import numpy as np
        NUM_HEADS = 16
        ROPE_THETA = 10000.0

        def _rope_cos_sin(head_dim, seq_len, theta=ROPE_THETA):
            exps = -jnp.arange(0, head_dim, 2)[:head_dim // 2].astype(jnp.float32) / head_dim
            freqs = theta ** exps
            ang = jnp.arange(seq_len, dtype=jnp.float32)[:, None] * freqs[None, :]
            return (jnp.cos(ang), jnp.sin(ang))

        def _apply_rope(x, cos, sin):
            x2 = x.reshape(*x.shape[:-1], -1, 2)
            xr, xi = (x2[..., 0], x2[..., 1])
            c = cos[None, None]
            s = sin[None, None]
            outr = xr * c - xi * s
            outi = xr * s + xi * c
            return jnp.stack([outr, outi], axis=-1).reshape(x.shape)
        B, S, D = x.shape
        H = NUM_HEADS
        hd = D // H
        q = (x @ Wq.T + bq).reshape(B, S, H, hd).transpose(0, 2, 1, 3)
        k = (x @ Wk.T + bk).reshape(B, S, H, hd).transpose(0, 2, 1, 3)
        v = (x @ Wv.T + bv).reshape(B, S, H, hd).transpose(0, 2, 1, 3)
        cos, sin = _rope_cos_sin(hd, S)
        q = _apply_rope(q, cos, sin)
        k = _apply_rope(k, cos, sin)
        inv_scale = 1.0 / jnp.sqrt(jnp.asarray(D, jnp.float32))
        scores = jax.nn.softmax(jnp.einsum('bhqd,bhkd->bhqk', q, k) * inv_scale, axis=-1)
        out = jnp.einsum('bhqk,bhkd->bhqd', scores, v)
        out = out.transpose(0, 2, 1, 3).reshape(B, S, D)
        return out @ Wo.T

    def _L0_ffn_ref(x, wqkv, q_scale, k_scale, wo, ln_g, ln_b, w1, b1, w2, b2):
        import jax, jax.numpy as jnp
        import numpy as np
        DIM = 256
        DEPTH = 2
        HEADS = 8
        DIM_HEAD = 64
        WINDOW = 128
        INNER = HEADS * DIM_HEAD
        HID = int(DIM * 4 * 2 / 3)
        B, N = (2, 2048)
        QK_SCALE = 8.0

        def shift_token(t):
            t1, t2 = jnp.split(t, 2, axis=-1)
            t2 = jnp.pad(t2, ((0, 0), (1, 0), (0, 0)))[:, :-1]
            return jnp.concatenate([t1, t2], axis=-1)

        def l2norm(t):
            return t / jnp.clip(jnp.linalg.norm(t, axis=-1, keepdims=True), 1e-12)

        def rotate_half(x):
            x1, x2 = jnp.split(x, 2, axis=-1)
            return jnp.concatenate([-x2, x1], axis=-1)

        def rotary_xpos(q, k):
            n = q.shape[-2]
            half_idx = jnp.arange(0, DIM_HEAD, 2, dtype=jnp.float32)
            inv_freq = 1.0 / 10000.0 ** (half_idx / DIM_HEAD)
            t = jnp.arange(n, dtype=jnp.float32)
            freqs = t[:, None] * inv_freq[None, :]
            freqs = jnp.concatenate([freqs, freqs], axis=-1)
            base = (half_idx + 0.4 * DIM_HEAD) / (1.4 * DIM_HEAD)
            power = (t - n // 2) / float(WINDOW // 2)
            scale = base[None, :] ** power[:, None]
            scale = jnp.concatenate([scale, scale], axis=-1)
            cos, sin = (jnp.cos(freqs), jnp.sin(freqs))
            q = q * cos * scale + rotate_half(q) * sin * scale
            k = k * cos / scale + rotate_half(k) * sin / scale
            return (q, k)

        def local_attention(q, k, v):
            b, h, n, d = q.shape
            w = n // WINDOW
            bq = q.reshape(b, h, w, WINDOW, d) * QK_SCALE
            bk = k.reshape(b, h, w, WINDOW, d)
            bv = v.reshape(b, h, w, WINDOW, d)

            def look_around(t):
                p = jnp.pad(t, ((0, 0), (0, 0), (1, 0), (0, 0), (0, 0)))
                return jnp.concatenate([p[:, :, :w], p[:, :, 1:]], axis=3)
            bk, bv = (look_around(bk), look_around(bv))
            bt = jnp.arange(n).reshape(w, WINDOW)
            btp = jnp.pad(bt, ((1, 0), (0, 0)), constant_values=-1)
            btk = jnp.concatenate([btp[:w], btp[1:]], axis=1)
            sim = jnp.einsum('bhwid,bhwjd->bhwij', bq, bk)
            i = bt[:, :, None]
            j = btk[:, None, :]
            mask = (i < j) | (i > j + WINDOW) | (j == -1)
            sim = jnp.where(mask, -jnp.finfo(sim.dtype).max, sim)
            attn = jax.nn.softmax(sim, axis=-1)
            out = jnp.einsum('bhwij,bhwjd->bhwid', attn, bv)
            return out.reshape(b, h, n, d)

        def _layer(x, wqkv, qs, ksc, wo, lg, lb, w1, b1, w2, b2):
            b, n, _ = x.shape
            h = shift_token(x)
            qkv = h @ wqkv
            q, k, v = jnp.split(qkv, 3, axis=-1)
            to_heads = lambda t: t.reshape(b, n, HEADS, DIM_HEAD).transpose(0, 2, 1, 3)
            q, k, v = (to_heads(q), to_heads(k), to_heads(v))
            q = l2norm(q) * qs
            k = l2norm(k) * ksc
            q, k = rotary_xpos(q, k)
            o = local_attention(q, k, v)
            o = o.transpose(0, 2, 1, 3).reshape(b, n, INNER)
            x = x + o @ wo
            h = shift_token(x)
            mu = h.mean(-1, keepdims=True)
            var = h.var(-1, keepdims=True)
            h = (h - mu) / jnp.sqrt(var + 1e-05) * lg + lb
            h = h @ w1 + b1
            a, g = jnp.split(h, 2, axis=-1)
            h = a * jax.nn.gelu(g, approximate=False)
            x = x + h @ w2 + b2
            return x
        for l in range(DEPTH):
            x = _layer(x, wqkv[l], q_scale[l], k_scale[l], wo[l], ln_g[l], ln_b[l], w1[l], b1[l], w2[l], b2[l])
        return x
    x = L0_attn_x
    x = _layernorm(x + _L0_attn_ref(x, L0_attn_Wq, L0_attn_bq, L0_attn_Wk, L0_attn_bk, L0_attn_Wv, L0_attn_bv, L0_attn_Wo), axis=-1)
    x = _layernorm(x + _L0_ffn_ref(x, L0_ffn_wqkv, L0_ffn_q_scale, L0_ffn_k_scale, L0_ffn_wo, L0_ffn_ln_g, L0_ffn_ln_b, L0_ffn_w1, L0_ffn_b1, L0_ffn_w2, L0_ffn_b2), axis=-1)
    return x

_drawn_inputs = setup_inputs


def setup_inputs(seed=0):
    import zlib

    import numpy as np

    out = dict(_drawn_inputs(seed))
    spreads = {'L0_ffn_q_scale': (1.0, 0.6),
     'L0_ffn_k_scale': (1.0, 0.6),
     'L0_ffn_ln_g': (1.0, 0.6),
     'L0_ffn_ln_b': (0.0, 0.8),
     'L0_ffn_b1': (0.0, 0.8),
     'L0_ffn_b2': (0.0, 0.1)}
    factors = {'L0_attn_Wq': 8.0,
     'L0_attn_bq': 8.0,
     'L0_attn_Wk': 8.0,
     'L0_attn_bk': 8.0,
     'L0_attn_Wv': 8.0,
     'L0_attn_bv': 8.0,
     'L0_attn_Wo': 7.865,
     'L0_ffn_wqkv': 3.361,
     'L0_ffn_wo': 3.311}
    for name, (base, spread) in spreads.items():
        noise = np.random.default_rng([zlib.crc32(name.encode()), seed]).standard_normal(out[name].shape)
        drawn = base * np.exp(spread * noise) if base else spread * noise
        out[name] = jnp.asarray(drawn.astype(out[name].dtype))
    for name, factor in factors.items():
        out[name] = (out[name] * factor).astype(out[name].dtype)
    return out
```

```python
from contextlib import ExitStack

import numpy as np
import concourse.bass as bass
from concourse import mybir

F32 = mybir.dt.float32
F32R = mybir.dt.float32r
BF16 = mybir.dt.bfloat16
ALU = mybir.AluOpType
ACT = mybir.ActivationFunctionType
AX = mybir.AxisListType

P = 128
B, S, D = 8, 1024, 256
T = S // P
KC = D // P
HALF = 512
LN_EPS = 1e-5

H1 = 16
HD1 = D // H1
GRP = 4
G = H1 // GRP
TERMS = 6
STACK = TERMS * HD1
MAXR = 2
VW = HD1 + 1
CYC = 2 * T
INV_SCALE = 1.0 / np.sqrt(float(D))


class Step:

    def __init__(self, kind, n=0, part=0, m=0, misc_now=0, t=0, par=0, g=0, slot=0, u=0, c=0, j=0, half=0, batch=0,
                 first=False):
        self.kind, self.n, self.part = kind, n, part
        self.m, self.misc_now = m, misc_now
        self.t, self.par, self.g, self.slot = t, par, g, slot
        self.u, self.c, self.j, self.half = u, c, j, half
        self.batch, self.first = batch, first


def plan_attention(section):
    steps, count = [], {}

    def add(kind, misc=False, **at):
        at["n"] = count.get(kind, 0)
        count[kind] = at["n"] + 1
        if misc:
            at["m"] = count.get("misc", 0)
            count["misc"] = at["m"] + 1
        at["misc_now"] = count.get("misc", 0)
        steps.append(Step(kind, **at))

    def project(t, par, part):
        if part == 0:
            add("x_transpose", True, t=t)
        if part == 1:
            add("qk_project", True, t=t, par=par)
        if part == 2:
            add("v_project", True, t=t, par=par)
            add("rope", t=t, par=par)

    def maxima(k, slot):
        add("row_max", slot=slot, j=k // T, t=k % T)

    if section == "prologue":
        add("load_x", batch=0, first=True)
        for t in range(T):
            for part in range(3):
                project(t, 0, part)
        add("load_x", batch=1, first=False)
        for g in range(2):
            for t in range(T):
                for kind in ("split_1", "rest_1", "split_2", "split_3"):
                    add(kind, t=t, par=0, g=g)
                add("stack", True, t=t, slot=g)
        for k in range(GRP * T):
            maxima(k, 0)
        add("max_hi")
        add("max_lo")
        add("max_rows", True, slot=0)
    if section == "body":
        for u in range(2 * G):
            par, g = u // G, u % G
            nxt = (u + 2) // G % 2, (u + 2) % G
            done = 0
            for c in range(CYC):
                if c == 0 and u in (2, 6):
                    add("load_x", batch=u // 2 + 1 if u == 2 else 3, first=False)
                if c == 0 and u in (1, 5):
                    add("load_residual", par=par, first=(u == 1))
                goal = min(GRP * T, -(-GRP * T * (c + 1) // (CYC - 4)))
                for j in range(GRP):
                    add("scores", u=u, c=c, j=j, slot=g)
                    if done < goal and (j != 1 or goal - done > 1):
                        maxima(done, (u + 1) % G)
                        done += 1
                    if c % 2 == 0:
                        add(("split_1", "rest_1", "split_2", "split_3")[j], t=c // 2, par=nxt[0], g=nxt[1])
                    if j == 0 and c in (2, 4):
                        add("divide", True, half=c // 2 - 1, u=(u - 1) % 2, par=(u - 1) // G % 2, g=(u - 1) % G)
                    if j == 1 and c in (2, 4):
                        add("divide_apply", half=c // 2 - 1, u=(u - 1) % 2, par=(u - 1) // G % 2, g=(u - 1) % G)
                    if j == 2 and c % 2 == 1:
                        add("stack", True, t=c // 2, slot=nxt[1])
                    if j == 1 and g < 2 and c % 4 < 2:
                        project(4 * g + c // 4, 1 - par, c % 4)
                    if j == 1 and g >= 2 and c % 4 == 1:
                        add("out_transpose", True, t=4 * (g - 2) + c // 4, par=1 - par)
                    if j == 1 and g >= 2 and c % 4 == 2:
                        add("out_project", True, t=4 * (g - 2) + c // 4, par=1 - par)
                    if g >= 2 and c % 4 == 2 and j > 1:
                        add(("norm_stats", "norm_mean")[j - 2])
                    if c == CYC - 4 and j in (0, 1):
                        add(("max_hi", "max_lo")[j])
                    if c == CYC - 4 and j == 3:
                        add("max_rows", True, slot=(u + 1) % G)
                    if j == 2 and g < 2 and c % 4 == 2:
                        project(4 * g + c // 4, 1 - par, 2)
                if c:
                    add("values", u=u, c=c - 1, par=par, g=g)
                elif u:
                    add("values", u=u - 1, c=CYC - 1, par=(u - 1) // G, g=(u - 1) % G)
                if g >= 2 and c % 4 == 3:
                    add("norm_apply", t=4 * (g - 2) + c // 4, par=1 - par)
        add("values", u=2 * G - 1, c=CYC - 1, par=1, g=G - 1)
    if section == "epilogue":
        for half in range(2):
            add("divide", True, half=half, u=1, par=1, g=G - 1)
            add("divide_apply", half=half, u=1, par=1, g=G - 1)
        for t in range(T):
            add("out_transpose", True, t=t, par=1)
            add("out_project", True, t=t, par=1)
            add("norm_stats")
            add("norm_mean")
            add("norm_apply", t=t, par=1)
    return steps


def attention_pass(nc, x, wqkv_t, bqkv, wo_t, rope_cos, rope_sin, ident_in, x1_scratch):
    with ExitStack() as ctx:
        def sb(name, shape, dt=F32):
            return ctx.enter_context(nc.sbuf_tensor(name, shape, dt))

        sems = []

        def sem(name):
            s = ctx.enter_context(nc.semaphore(name))
            sems.append(s)
            return s

        psum = ctx.enter_context(nc.psum_tensor("a_psum", [P, 8, HALF], F32))
        max_banks = [psum[:, 0:2, :], psum[:, 2:4, :]]
        score_banks = [psum[:, 4, :], psum[:, 5, :]]
        value_bank = psum[:, 6, :]
        misc_bank = psum[:, 7, :]
        misc_half = misc_bank.bitcast(BF16)

        w_qkv = sb("a_wqkv", [P, KC, 3 * D])
        w_out = sb("a_wo", [P, KC, D])
        bias = sb("a_bias", [P, 3 * D])
        ident = sb("a_ident", [P, P])
        cos_t = sb("a_cos", [P, T, HD1])
        sin_t = sb("a_sin", [P, T, HD1])
        x_in = sb("a_x_in", [P, T, D])
        x_res = sb("a_x_res", [P, 2, T, D])
        x_tr = sb("a_x_tr", [P, KC, P])
        qk = sb("a_qk", [P, 2 * D])
        by_cos = sb("a_by_cos", [P, 2 * D])
        by_sin = sb("a_by_sin", [P, 2 * D])
        rest = sb("a_rest", [P, 2, GRP, HD1])
        roped = sb("a_roped", [P, 2, T, 2 * D])
        v_ones = sb("a_v_ones", [P, 2, T, H1, VW])
        source = sb("a_source", [P, 2, 2, GRP, P], BF16)
        stacks = sb("a_stacks", [P, G, 2, GRP, S], BF16)
        row_max = sb("a_row_max", [P, GRP, T])
        max_terms = sb("a_max_terms", [P, GRP, MAXR, T], BF16)
        max_row = sb("a_max_row", [GRP * MAXR * T, P], BF16)
        ident_b = sb("a_ident_b", [P, P], BF16)
        probs = sb("a_probs", [P, 2 * GRP, HALF])
        values_tr = sb("a_values_tr", [P, 2, S])
        recip = sb("a_recip", [P, 2, 4, GRP])
        attn = sb("a_attn", [P, 2, T, D])
        attn_tr = sb("a_attn_tr", [P, KC, P])
        res = sb("a_res", [P, 2, D])
        stats = sb("a_stats", [P, 2, 6])
        mean_var = sb("a_mean_var", [P, 2, 2])
        var_eps = sb("a_var_eps", [P, 2, 1])
        rstd = sb("a_rstd", [P, 2, 1])
        minus_half = sb("a_minus_half", [P, 1])
        x1_out = sb("a_x1_out", [P, 2, D])

        constants_loaded = sem("a_constants_loaded")
        preset = sem("a_preset")
        x_loaded = sem("a_x_loaded")
        residual_loaded = sem("a_residual_loaded")
        misc_filled = sem("a_misc_filled")
        misc_taken = sem("a_misc_taken")
        cos_done = sem("a_cos_done")
        sin_done = sem("a_sin_done")
        roped_done = sem("a_roped_done")
        hi_done = sem("a_hi_done")
        lo_done = sem("a_lo_done")
        dup_done = sem("a_dup_done")
        rest_done = sem("a_rest_done")
        mid_done = sem("a_mid_done")
        max_hi = sem("a_max_hi")
        max_lo = sem("a_max_lo")
        max_scores = sem("a_max_scores")
        max_taken = sem("a_max_taken")
        max_row_stored = sem("a_max_row_stored")
        scores_ready = sem("a_scores_ready")
        probs_ready = sem("a_probs_ready")
        values_done = sem("a_values_done")
        values_copied = sem("a_values_copied")
        recip_done = sem("a_recip_done")
        stats_done = sem("a_stats_done")
        mean_done = sem("a_mean_done")
        eps_done = sem("a_eps_done")
        rstd_done = sem("a_rstd_done")
        x1_ready = sem("a_x1_ready")
        x1_stored = [sem(f"a_x1_stored_{k}") for k in range(2)]

        x_t = x.rearrange("b (t p) d -> b p t d", p=P)
        slots_t = x1_scratch.rearrange("b (t p) d -> b p t d", p=P)

        def heads(ap, n):
            return ap.rearrange("p (h d) -> p h d", h=n)

        value_sums = misc_bank.rearrange("p (k j d) -> p k j d", k=4, j=GRP)

        def terms(k):
            return source[:, k, :, :, 0:STACK].rearrange("p w j (e d) -> p w j e d", e=TERMS)

        def section(name, i=None):
            steps = plan_attention(name)
            stack_m = [s.m for s in steps if s.kind == "stack"]
            max_m = [s.m for s in steps if s.kind == "max_rows"]
            stack_ready = {}
            rows = 0
            for s in steps:
                if s.kind in ("row_max", "scores"):
                    s.stack_need, s.rows_need = stack_ready.get(s.slot, 0), rows
                if s.kind == "stack":
                    stack_ready[s.slot] = s.m + 1
                if s.kind == "max_rows":
                    rows += 16 * GRP

            with nc.Block() as block:
                @block.sync
                def _(sp):
                    for s in steps:
                        if s.kind == "load_x":
                            if s.misc_now and not s.first:
                                sp.wait_ge(misc_filled, s.misc_now)
                            src = x_t[s.batch] if i is None else x_t[(2 * i + s.batch) % B]
                            sp.dma_start(x_in[:], src).then_inc(x_loaded, 16)
                        if s.kind == "load_residual":
                            if not s.first:
                                sp.wait_ge(misc_taken, s.misc_now)
                            sp.dma_start(x_res[:, s.par], x_t[2 * i + s.par]).then_inc(residual_loaded, 16)
                        if s.kind == "max_rows":
                            sp.wait_ge(misc_taken, s.m + 1)
                            for j in range(GRP):
                                dst = stacks[STACK:STACK + MAXR, s.slot, 0, j, :].rearrange("p (t q) -> p t q", t=T)
                                sp.dma_start(dst, max_row[j * MAXR * T:(j + 1) * MAXR * T, :]).then_inc(max_row_stored, 16)
                        if s.kind == "norm_apply":
                            sp.wait_ge(x1_ready, s.n + 1)
                            slot = B if i is None else 2 * i + 1 - s.par
                            sp.dma_start(slots_t[slot][:, s.t, :], x1_out[:, s.n % 2]).then_inc(x1_stored[s.n % 2], 16)
                    stores = sum(s.kind == "norm_apply" for s in steps)
                    for k in range(2):
                        if stores:
                            sp.wait_ge(x1_stored[k], 16 * (stores // 2))
                    for kind, done in (("load_x", x_loaded), ("load_residual", residual_loaded)):
                        n = sum(s.kind == kind for s in steps)
                        if n:
                            sp.wait_ge(done, 16 * n)
                    if rows:
                        sp.wait_ge(max_row_stored, rows)

                @block.tensor
                def _(pe):
                    for s in steps:
                        if s.kind in ("x_transpose", "qk_project", "v_project", "stack", "max_rows",
                                      "divide", "out_transpose", "out_project") and s.m:
                            pe.wait_ge(misc_taken, s.m)
                        if s.kind == "x_transpose":
                            if name == "prologue":
                                pe.wait_ge(x_loaded, 16)
                            elif s.n >= T:
                                pe.wait_ge(x_loaded, 16)
                            for k in range(KC):
                                ins = pe.transpose(misc_bank[:, k * P:(k + 1) * P], x_in[:, s.t, k * P:(k + 1) * P],
                                                   ident[:])
                            ins.then_inc(misc_filled, 1)
                        if s.kind == "qk_project":
                            for k in range(KC):
                                ins = pe.matmul(misc_bank[:, 0:2 * D], x_tr[:, k, :], w_qkv[:, k, 0:2 * D],
                                                start=(k == 0), stop=(k == KC - 1))
                            ins.then_inc(misc_filled, 1)
                        if s.kind == "v_project":
                            for k in range(KC):
                                ins = pe.matmul(misc_bank[:, 0:D], x_tr[:, k, :], w_qkv[:, k, 2 * D:3 * D],
                                                start=(k == 0), stop=(k == KC - 1))
                            ins.then_inc(misc_filled, 1)
                        if s.kind == "stack":
                            pe.wait_ge(lo_done, 2 * (s.n + 1))
                            pe.wait_ge(dup_done, 4 * (s.n + 1))
                            for w in range(2 * GRP):
                                ins = pe.transpose(misc_half[:, w * P:(w + 1) * P],
                                                   source[:, s.n % 2, w // GRP, w % GRP, :], ident_b[:])
                            ins.then_inc(misc_filled, 1)
                        if s.kind == "row_max":
                            if s.stack_need:
                                pe.wait_ge(misc_taken, s.stack_need)
                            if s.n >= 2:
                                pe.wait_ge(max_taken, s.n - 1)
                            q = stacks[0:STACK, s.slot, 0, s.j, s.t * P:(s.t + 1) * P]
                            for h in range(2):
                                k_rows = stacks[0:STACK, s.slot, 1, s.j, h * HALF:(h + 1) * HALF]
                                ins = pe.matmul(max_banks[s.n % 2][:, h, :], q, k_rows, start=True, stop=True)
                            ins.then_inc(max_scores, 1)
                        if s.kind == "max_rows":
                            pe.wait_ge(max_lo, s.n + 1)
                            pe.transpose(misc_half[0:GRP * MAXR * T, 0:P], max_terms.rearrange("p a b c -> p (a b c)"),
                                         ident_b[:]).then_inc(misc_filled, 1)
                        if s.kind == "scores":
                            if s.rows_need:
                                pe.wait_ge(max_row_stored, s.rows_need)
                            if s.n >= 2:
                                pe.wait_ge(probs_ready, s.n - 1)
                            half, t = s.c // T, s.c % T
                            k_rows = stacks[0:STACK + MAXR, s.slot, 1, s.j, t * P:(t + 1) * P]
                            q = stacks[0:STACK + MAXR, s.slot, 0, s.j, half * HALF:(half + 1) * HALF]
                            pe.matmul(score_banks[s.n % 2], k_rows, q, start=True, stop=True).then_inc(scores_ready, 1)
                        if s.kind == "values":
                            t = s.c % T
                            pe.wait_ge(probs_ready, GRP * (s.n + 1))
                            if t == 0 and s.n >= T:
                                pe.wait_ge(values_copied, s.n // T)
                            for j in range(GRP):
                                ins = pe.matmul(value_bank[32 * j:32 * j + VW, :], v_ones[:, s.par, t, s.g * GRP + j, :],
                                                probs[:, GRP * (s.n % 2) + j, :], start=(t == 0), stop=(t == T - 1))
                            ins.then_inc(values_done, 1)
                        if s.kind == "divide":
                            if name == "body" and s.n >= 2:
                                pe.wait_ge(values_copied, s.n - 1)
                            for k in range(4):
                                q0 = (4 * s.half + k) * P
                                ins = pe.transpose(misc_bank[:, k * P:(k + 1) * P], values_tr[:, s.u, q0:q0 + P], ident[:])
                            ins.then_inc(misc_filled, 1)
                        if s.kind == "out_transpose":
                            for k in range(KC):
                                ins = pe.transpose(misc_bank[:, k * P:(k + 1) * P], attn[:, s.par, s.t, k * P:(k + 1) * P],
                                                   ident[:])
                            ins.then_inc(misc_filled, 1)
                        if s.kind == "out_project":
                            for k in range(KC):
                                ins = pe.matmul(misc_bank[:, 0:D], attn_tr[:, k, :], w_out[:, k, :],
                                                start=(k == 0), stop=(k == KC - 1))
                            ins.then_inc(misc_filled, 1)

                @block.scalar
                def _(act):
                    for s in steps:
                        if s.kind == "x_transpose":
                            act.wait_ge(misc_filled, s.m + 1)
                            act.copy(x_tr[:], misc_bank[:, 0:D].rearrange("p (k q) -> p k q", k=KC))\
                               .then_inc(misc_taken, 1)
                        if s.kind == "stack":
                            act.wait_ge(misc_filled, s.m + 1)
                            act.copy(stacks[:, s.slot, :, :, s.t * P:(s.t + 1) * P].rearrange("p w j q -> p (w j) q"),
                                     misc_half.rearrange("p (w q) -> p w q", w=2 * GRP)).then_inc(misc_taken, 1)
                        if s.kind == "max_rows":
                            act.wait_ge(misc_filled, s.m + 1)
                            if s.n:
                                act.wait_ge(max_row_stored, 16 * GRP * s.n)
                            act.copy(max_row[:], misc_half[0:GRP * MAXR * T, 0:P]).then_inc(misc_taken, 1)
                        if s.kind == "scores":
                            act.wait_ge(scores_ready, s.n + 1)
                            if s.n >= 2 * GRP:
                                act.wait_ge(values_done, s.n // GRP - 1)
                            act.activation(probs[:, s.n % (2 * GRP)], score_banks[s.n % 2], ACT.Exp,
                                           scale=float(INV_SCALE)).then_inc(probs_ready, 1)
                        if s.kind == "values" and s.c % T == T - 1:
                            half = s.c // T
                            act.wait_ge(values_done, s.n + 1)
                            act.copy(values_tr[:, s.u % 2, half * HALF:(half + 1) * HALF], value_bank)\
                               .then_inc(values_copied, 1)
                        if s.kind == "out_transpose":
                            act.wait_ge(misc_filled, s.m + 1)
                            act.copy(attn_tr[:], misc_bank[:, 0:D].rearrange("p (k q) -> p k q", k=KC))\
                               .then_inc(misc_taken, 1)

                @block.vector
                def _(dve):
                    roped_at = {}
                    for s in steps:
                        if s.kind == "qk_project":
                            dve.wait_ge(misc_filled, s.m + 1)
                            if s.n:
                                dve.wait_ge(cos_done, s.n)
                                dve.wait_ge(sin_done, 2 * s.n)
                            dve.tensor_tensor(qk[:], misc_bank[:, 0:2 * D], bias[:, 0:2 * D], ALU.add)\
                               .then_inc(misc_taken, 1)
                            qk_m = s.m
                        if s.kind == "v_project":
                            dve.wait_ge(misc_filled, s.m + 1)
                            dve.tensor_tensor(v_ones[:, s.par, s.t, :, 0:HD1], heads(misc_bank[:, 0:D], H1),
                                              heads(bias[:, 2 * D:3 * D], H1), ALU.add).then_inc(misc_taken, 1)
                        if s.kind == "rope":
                            roped_at[s.par, s.t] = s.n + 1
                        if s.kind in ("split_1", "rest_1", "split_2", "split_3"):
                            rq = roped[:, s.par, s.t, :].rearrange("p (w h d) -> p w h d", w=2, h=H1)
                            rq = rq[:, :, s.g * GRP:(s.g + 1) * GRP, :]
                            src = terms(s.n % 2)
                        if s.kind == "split_1":
                            if (s.par, s.t) in roped_at:
                                dve.wait_ge(roped_done, roped_at[s.par, s.t])
                            if s.n >= 2:
                                dve.wait_ge(misc_filled, stack_m[s.n - 2] + 1)
                            dve.tensor_copy(src[:, :, :, 0, :], rq).then_inc(hi_done, 1)
                        if s.kind == "rest_1":
                            dve.wait_ge(hi_done, s.n + 1)
                            dve.tensor_tensor(rest[:], rq, src[:, :, :, 0, :], ALU.subtract).then_inc(rest_done, 1)
                        if s.kind == "split_2":
                            dve.wait_ge(rest_done, s.n + 1)
                            for w, at in enumerate((3, 1)):
                                dve.tensor_copy(src[:, w, :, at, :], rest[:, w]).then_inc(mid_done, 1)
                        if s.kind == "split_3":
                            dve.wait_ge(mid_done, 2 * (s.n + 1))
                            for w, (at, mid) in enumerate(((5, 3), (2, 1))):
                                dve.tensor_tensor(src[:, w, :, at, :], rest[:, w], src[:, w, :, mid, :], ALU.subtract)\
                                   .then_inc(lo_done, 1)
                        if s.kind == "row_max":
                            dve.wait_ge(max_scores, s.n + 1)
                            dve.tensor_reduce(row_max[:, s.j, s.t:s.t + 1], max_banks[s.n % 2], AX.XY, ALU.max, negate=True)\
                               .then_inc(max_taken, 1)
                        if s.kind == "max_hi":
                            dve.wait_ge(max_taken, GRP * T * (s.n + 1))
                            if s.n:
                                dve.wait_ge(misc_filled, max_m[s.n - 1] + 1)
                            dve.tensor_copy(max_terms[:, :, 0, :], row_max[:]).then_inc(max_hi, 1)
                        if s.kind == "max_lo":
                            dve.wait_ge(max_hi, s.n + 1)
                            dve.tensor_tensor(max_terms[:, :, 1, :], row_max[:], max_terms[:, :, 0, :], ALU.subtract)\
                               .then_inc(max_lo, 1)
                        if s.kind == "divide":
                            dve.wait_ge(misc_filled, s.m + 1)
                            dve.reciprocal(recip[:, s.n % 2], value_sums[:, :, :, HD1]).then_inc(recip_done, 1)
                        if s.kind == "divide_apply":
                            dve.wait_ge(recip_done, s.n + 1)
                            out = attn[:, s.par, 4 * s.half:4 * s.half + 4, s.g * GRP * HD1:(s.g + 1) * GRP * HD1]
                            dve.tensor_tensor(out.rearrange("p k (j d) -> p k j d", j=GRP), value_sums[:, :, :, 0:HD1],
                                              recip[:, s.n % 2].unsqueeze(3).to_broadcast([P, 4, GRP, HD1]), ALU.mult)\
                               .then_inc(misc_taken, 1)
                        if s.kind == "out_project":
                            dve.wait_ge(misc_filled, s.m + 1)
                            if i is not None and s.par == 0:
                                dve.wait_ge(residual_loaded, 16)
                            dve.tensor_tensor(res[:, s.n % 2], misc_bank[:, 0:D], x_res[:, s.par, s.t, :], ALU.add)\
                               .then_inc(misc_taken, 1)
                            res_m = s.m
                        if s.kind == "norm_stats":
                            dve.wait_ge(misc_taken, res_m + 1)
                            dve.bn_stats(stats[:, s.n % 2], res[:, s.n % 2]).then_inc(stats_done, 1)
                        if s.kind == "norm_mean":
                            dve.wait_ge(stats_done, s.n + 1)
                            if s.n >= 2:
                                dve.wait_ge(eps_done, s.n - 1)
                            dve.bn_aggr(mean_var[:, s.n % 2], stats[:, s.n % 2]).then_inc(mean_done, 1)
                        if s.kind == "norm_apply":
                            dve.wait_ge(rstd_done, s.n + 1)
                            if s.n >= 2:
                                dve.wait_ge(x1_stored[s.n % 2], 16 * (s.n // 2))
                            dve.tensor_scalar(x1_out[:, s.n % 2], res[:, s.n % 2], mean_var[:, s.n % 2, 0:1],
                                              rstd[:, s.n % 2], ALU.subtract, ALU.mult).then_inc(x1_ready, 1)

                @block.gpsimd
                def _(pool):
                    for s in steps:
                        if s.kind == "qk_project":
                            qk_m = s.m
                        if s.kind == "rope":
                            pool.wait_ge(misc_taken, qk_m + 1)
                            if s.n:
                                pool.wait_ge(roped_done, s.n)
                            table = cos_t[:, s.t, :].unsqueeze(1).to_broadcast([P, 2 * H1, HD1])
                            pool.tensor_tensor(heads(by_cos[:], 2 * H1), heads(qk[:], 2 * H1), table,
                                               ALU.mult).then_inc(cos_done, 1)
                            pairs = qk[:].rearrange("p (h e two) -> p h e two", h=2 * H1, two=2)
                            outs = by_sin[:].rearrange("p (h e two) -> p h e two", h=2 * H1, two=2)
                            sins = sin_t[:, s.t, :].rearrange("p (e two) -> p e two", two=2)
                            for e in range(2):
                                table = sins[:, :, e].unsqueeze(1).to_broadcast([P, 2 * H1, HD1 // 2])
                                pool.tensor_tensor(outs[:, :, :, e], pairs[:, :, :, 1 - e], table, ALU.mult)\
                                    .then_inc(sin_done, 1)
                            pool.wait_ge(cos_done, s.n + 1)
                            pool.wait_ge(sin_done, 2 * (s.n + 1))
                            pool.tensor_tensor(roped[:, s.par, s.t, :], by_cos[:], by_sin[:], ALU.add)\
                                .then_inc(roped_done, 1)
                        if s.kind == "split_1":
                            pool.wait_ge(hi_done, s.n + 1)
                            src = terms(s.n % 2)
                            for w, at in enumerate((slice(1, 3), slice(3, 6, 2))):
                                first = src[:, w, :, 0:1, :].to_broadcast([P, GRP, 2, HD1])
                                pool.tensor_copy(src[:, w, :, at, :], first).then_inc(dup_done, 1)
                        if s.kind == "split_2":
                            src = terms(s.n % 2)
                            pool.wait_ge(mid_done, 2 * (s.n + 1))
                            for w, mid in enumerate((3, 1)):
                                pool.tensor_copy(src[:, w, :, 4, :], src[:, w, :, mid, :]).then_inc(dup_done, 1)
                        if s.kind == "norm_mean":
                            pool.wait_ge(mean_done, s.n + 1)
                            if s.n >= 2:
                                pool.wait_ge(x1_ready, s.n - 1)
                            pool.tensor_scalar(var_eps[:, s.n % 2], mean_var[:, s.n % 2, 1:2], LN_EPS, None, ALU.add)\
                                .then_inc(eps_done, 1)
                            pool.wait_ge(eps_done, s.n + 1)
                            pool.tensor_tensor(rstd[:, s.n % 2], var_eps[:, s.n % 2], minus_half[:], ALU.pow)\
                                .then_inc(rstd_done, 1)

            nc.all_engine_barrier(sems_to_clear=range(min(sem_nums), max(sem_nums) + 1))

        sem_nums = [s.num for s in sems]

        with nc.Block() as block:
            @block.sync
            def _(sp):
                sp.dma_start(w_qkv[:], wqkv_t.rearrange("(k p) n -> p k n", p=P)).then_inc(constants_loaded, 16)
                sp.dma_start(w_out[:], wo_t.rearrange("(k p) n -> p k n", p=P)).then_inc(constants_loaded, 16)
                sp.dma_start(bias[:], bqkv.partition_broadcast(P)).then_inc(constants_loaded, 16)
                sp.dma_start(cos_t[:], rope_cos.rearrange("(t p) e -> p t e", p=P)).then_inc(constants_loaded, 16)
                sp.dma_start(sin_t[:], rope_sin.rearrange("(t p) e -> p t e", p=P)).then_inc(constants_loaded, 16)
                sp.dma_start(ident[:], ident_in).then_inc(constants_loaded, 16)
                sp.wait_ge(constants_loaded, 96)

            @block.vector
            def _(dve):
                dve.memset(value_bank, 0.0)
                dve.memset(source[:, :, :, :, STACK:P], 0.0).then_inc(preset, 1)
                dve.wait_ge(preset, 1)
                dve.memset(source[:, :, 1, :, STACK:STACK + MAXR], 1.0)
                dve.wait_ge(constants_loaded, 96)
                dve.tensor_copy(ident_b[:], ident[:])
                dve.memset(minus_half[:], -0.5)

            @block.gpsimd
            def _(pool):
                pool.memset(v_ones[:, :, :, :, HD1:VW], 1.0)
                pool.memset(x_res[:, 1], 0.0)
                pool.memset(values_tr[:, 1], 1.0)
                pool.memset(attn[:, 1], 0.0)
        section("prologue")
        with nc.Fori(0, B // 2) as i:
            section("body", i)
        section("epilogue")


H2 = 8
HD2 = 64
INNER = H2 * HD2
WINDOW = 128
HID = int(D * 4 * 2 / 3)
HCH = 6
HCW = -(-HID // HCH)
OC = INNER // P
MGRP = 4
BODY = 2 * T
DEPTH = 2
QK_SCALE = 8.0
MASKED = -1e37



def plan_layer(section, last):
    steps = []
    low, high = (0 if section == "first" else -BODY), (0 if section == "last" else 2 * BODY)

    def add(kind, n, part=0):
        if low <= n < high:
            steps.append(Step(kind, n=n, part=part))

    if section == "first":
        for n in range(5):
            add("load", n)
        add("h_transpose", 0)
    for s in range(BODY if section != "last" else MGRP + 10):
        group, phase = (s - 9) // MGRP * MGRP, (s - 9) % MGRP
        early = [("mlp_in", group, 3 * phase + c) for c in range(3)] if phase < 2 else \
            [("mlp_out", group + 2 * (phase - 2) + c, 0) for c in range(2)] + [None]
        if last and phase == 1:
            add("load_x1", group)
            add("load_x1", group + 1)
        add("load", s + 5)
        add("turn_q", s - 1)
        add("wo", s - 3)
        add("turn_k", s - 1)
        add("p_transpose", s - 2, 0)
        add("h_transpose", s + 1)
        add("project_q", s)
        add("window_scores", s - 1, 0)
        add("attend", s - 2, 0)
        add("p_transpose", s - 2, 1)
        add("window_scores", s - 1, 1)
        add("scale", s - 1, 0)
        add("project_k", s)
        add("rope", s)
        add("attend", s - 2, 1)
        if phase >= 2:
            add(*early[0])
        add("p_transpose", s - 2, 2)
        add("window_scores", s - 1, 2)
        add("scale", s - 1, 1)
        add("y_transpose", s - 3)
        add("project_v", s)
        add("attend", s - 2, 2)
        add("p_transpose", s - 2, 3)
        add("window_scores", s - 1, 3)
        add("scale", s - 1, 2)
        if phase >= 2:
            add(*early[1])
        add("y_shift", s - 4)
        add("scale", s - 1, 3)
        add("attend", s - 2, 3)
        add("o_split", s - 2)
        add("ln_transpose", s - 5)
        if phase < 2:
            for piece in early:
                add(*piece)
        add("ln_apply", s - 4)
        if phase >= 2:
            for c in range(2):
                add("finish_mean", group + 2 * (phase - 2) + c)
            for c in range(2):
                add("finish", group + 2 * (phase - 2) + c)
            if last and phase == 2:
                add("load_x1", group + 2)
                add("load_x1", group + 3)
    return steps


SMALL_USES = ("h_transpose", "y_transpose", "y_shift", "ln_transpose")
OUT_USES = ("project_v", "wo", "mlp_out")
TURN_USES = ("turn_q", "turn_k", "p_transpose")


def layer_pass(nc, layer, last, x_src, x1_src, dst, wqkv, q_scale, k_scale, wo, ln_g, ln_b, w1, b1, w2, b2,
               tables, mask_in, ident_in):
    with ExitStack() as ctx:
        def sb(name, shape, dt=F32):
            return ctx.enter_context(nc.sbuf_tensor(f"l{layer}_{name}", shape, dt))

        sems = []

        def sem(name):
            s = ctx.enter_context(nc.semaphore(f"l{layer}_{name}"))
            sems.append(s)
            return s

        psum = ctx.enter_context(nc.psum_tensor(f"l{layer}_psum", [P, 8, HALF], F32))
        qk_banks = psum[:, 0:2, :]
        out_bank = psum[:, 2, :]
        small_bank = psum[:, 3, :]
        pair_banks = [psum[:, 4, :], psum[:, 5, :]]
        turn_bank = psum[:, 6, :]
        attend_bank = psum[:, 7, :]

        wqkv_t = [sb(f"wqkv_{k}", [P, KC, 3 * INNER], F32R) for k in range(2)]
        wo_t = [sb(f"wo_{k}", [P, OC, D], F32R) for k in range(2)]
        w1_t = [sb(f"w1_{k}", [P, KC, 2 * HID], F32R) for k in range(2)]
        w2_t = [sb(f"w2_{k}", [HCW, HCH, D], F32R) for k in range(2)]
        mask = sb("mask", [P, 2, 2, 2 * P], BF16)
        ident = sb("ident", [P, P])
        ident_b = sb("ident_b", [P, P], BF16)
        rope_c = sb("rope_c", [P, T, 2, HD2])
        rope_s = sb("rope_s", [P, T, 2, HD2])
        gain = sb("gain", [P, KC])
        shift = sb("shift", [P, KC])
        b1_a = sb("b1_a", [HCW, HCH])
        b1_g = sb("b1_g", [HCW, HCH])
        b2_all = sb("b2_all", [P, D])
        scales = sb("scales", [P, 2, HD2])
        exponent = sb("exponent", [P, 2 * H2])
        zero_col = sb("zero_col", [P, 1])
        x = sb("x", [P, T, D])
        y = sb("y", [P, 2 * T, D])
        h_t = [sb(f"h_t_{k}", [P, 2, KC, P + 1], F32R) for k in range(2)]
        work_a = sb("work_a", [P, 2, H2, HD2])
        work_b = sb("work_b", [P, 2, H2, HD2])
        rot = sb("rot", [P, 2 * INNER])
        squares_sum = sb("squares_sum", [P, 2, 2 * H2])
        clipped = sb("clipped", [P, 2, 2 * H2])
        inv_norm = sb("inv_norm", [P, 2, 2 * H2])
        q_t = sb("q_t", [P, OC, P])
        k_t = sb("k_t", [P, 4, OC, P])
        v = sb("v", [P, 4, INNER])
        probs = sb("probs", [P, H2, 2 * P])
        neg_max = sb("neg_max", [P, 2, H2])
        sums = sb("sums", [P, 2, H2])
        inv_sums = sb("inv_sums", [P, 2, H2])
        probs_t = sb("probs_t", [P, 2, 4, P])
        o_t = [sb(f"o_t_{k}", [P, OC, P], F32R) for k in range(2)]
        y_t = sb("y_t", [P, 2, P + 1])
        normed = sb("normed", [P, 2, D])
        stats = sb("stats", [P, 2, 2, 6])
        mean_var = sb("mean_var", [P, 2, 2])
        var_eps = sb("var_eps", [P, 2, 1])
        rstd = sb("rstd", [P, 2, 1])
        ln_full = sb("ln_full", [P, KC, P])
        ln_t = [sb(f"ln_t_{k}", [P, 2, KC, MGRP * P], F32R) for k in range(2)]
        gate = sb("gate", [HCW, MGRP * P])
        hid_full = sb("hid_full", [HCW, MGRP * P])
        hid = [sb(f"hid_{k}", [HCW, HCH, MGRP * P], F32R) for k in range(2)]
        x_out = sb("x_out", [P, 2, D])
        x1_in = sb("x1_in", [P, 2, D]) if last else None
        f_stats = sb("f_stats_t", [P, 2, 6])
        f_mean_var = sb("f_mean_var", [P, 2, 2])
        f_var_eps = sb("f_var_eps", [P, 2, 1])
        f_rstd = sb("f_rstd", [P, 2, 1])

        constants_loaded = sem("constants_loaded")
        stage_loaded = [sem(f"stage_loaded_{k}") for k in range(2)]
        stage_hi = sem("stage_hi")
        stage_lo = sem("stage_lo")
        preset = sem("preset")
        x_loaded = [sem(f"x_loaded_{k}") for k in range(T)]
        small_filled, small_taken = sem("small_filled"), sem("small_taken")
        out_filled, out_taken = sem("out_filled"), sem("out_taken")
        turn_filled, turn_taken = sem("turn_filled"), sem("turn_taken")
        h_hi, h_lo = sem("h_hi"), sem("h_lo")
        q_ready, k_ready = sem("q_ready"), sem("k_ready")
        squared = sem("squared")
        squares_summed = sem("squares_summed")
        norms_clipped, norms_ready = sem("norms_clipped"), sem("norms_ready")
        by_cos_done, by_sin_done = sem("by_cos_done"), sem("by_sin_done")
        rope_added, rotated = sem("rope_added"), sem("rotated")
        pair_filled = sem("pair_filled")
        max_done = sem("max_done")
        exp_done = sem("exp_done")
        sums_inverted = sem("sums_inverted")
        probs_scaled = sem("probs_scaled")
        attend_done = sem("attend_done")
        o_hi, o_lo = sem("o_hi"), sem("o_lo")
        y_t_done = sem("y_t_done")
        shifted = sem("shifted")
        y_stats, y_mean, y_eps, y_rstd, y_normed = (sem(k) for k in ("y_stats", "y_mean", "y_eps", "y_rstd", "y_normed"))
        ln_hi, ln_lo = sem("ln_hi"), sem("ln_lo")
        y_biased = sem("y_biased")
        gated = sem("gated")
        hid_product, hid_hi, hid_lo = sem("hid_product"), sem("hid_hi"), sem("hid_lo")
        x1_loaded = [sem(f"x1_loaded_{k}") for k in range(2)]
        f_summed, f_stats_done, f_mean, f_eps, f_rstd_done = (
            sem(k) for k in ("f_summed", "f_stats", "f_mean", "f_eps", "f_rstd_done"))
        x_out_ready = sem("x_out_ready")
        stored = [sem(f"stored_{k}") for k in range(2)]

        def tile_of(dram, i, n):
            flat = dram.rearrange("b (t p) d -> (b t) p d", p=P)
            tile = BODY * i + n
            return flat[tile % (B * T) if n >= BODY else tile]

        def three(eng, out, left, right, first, final):
            eng.matmul(out, left[0], right[0], start=first, stop=False)
            eng.matmul(out, left[0], right[1], start=False, stop=False)
            return eng.matmul(out, left[1], right[0], start=False, stop=final)

        def section(name, i):
            steps = plan_layer(name, last)
            counts, made, used, pair_uses, loaded = {}, {}, {}, [], {}
            for s in steps:
                counts[s.kind] = counts.get(s.kind, 0) + 1
                s.count = made[s.kind, s.n, s.part] = counts[s.kind]
                for bank, kinds in (("small", SMALL_USES), ("out", OUT_USES), ("turn", TURN_USES)):
                    if s.kind in kinds:
                        s.use = counts.get(bank, 0)
                        counts[bank] = used[s.kind, s.n, s.part] = s.use + 1
                if s.kind == "window_scores":
                    s.pair = len(pair_uses)
                    pair_uses.append((exp_done, 2 * s.count))
                if s.kind == "mlp_in":
                    s.pair = len(pair_uses)
                    pair_uses += [(hid_product, s.count), (gated, s.count)]
                if s.kind == "load":
                    loaded[s.n] = 16 * (1 + sum(m % T == s.n % T for m in loaded))

            def after(eng, semaphore, kind, n, part=0, per=1):
                if (kind, n, part) in made:
                    eng.wait_ge(semaphore, per * made[kind, n, part])

            def after_use(eng, semaphore, kind, n, part=0):
                if (kind, n, part) in used:
                    eng.wait_ge(semaphore, used[kind, n, part])

            def windows(t):
                return (0, 1) if t else (1,)

            def place(part, h):
                return slice(part % 2 * HD2, (part % 2 + 1) * HD2), part // 2 * 2 + h

            def take_probs(eng, copy, s):
                t = s.n % T
                eng.wait_ge(turn_filled, s.use + 1)
                before = (s.n, s.part - 2) if s.part >= 2 else (s.n - 1, s.part + 2)
                after(eng, attend_done, "attend", *before)
                src = turn_bank.rearrange("p (h w q) -> p h w q", h=2, w=2)
                out = probs_t[:, s.part % 2].rearrange("p (h w) q -> p h w q", h=2)
                if t:
                    copy(out, src).then_inc(turn_taken, 1)
                else:
                    copy(out[:, :, 1, :], src[:, :, 1, :]).then_inc(turn_taken, 1)

            with nc.Block() as block:
                @block.sync
                def _(sp):
                    for s in steps:
                        if s.kind == "load":
                            after_use(sp, out_taken, "wo", s.n - T)
                            sp.dma_start(x[:, s.n % T, :], tile_of(x_src, i, s.n)).then_inc(x_loaded[s.n % T], 16)
                        if s.kind == "load_x1":
                            after(sp, f_summed, "mlp_out", s.n - 2)
                            sp.dma_start(x1_in[:, s.n % 2], tile_of(x1_src, i, s.n)).then_inc(x1_loaded[s.n % 2], 16)
                        if s.kind == "finish":
                            if last:
                                sp.wait_ge(x_out_ready, s.count)
                            else:
                                after_use(sp, out_taken, "mlp_out", s.n)
                            sp.dma_start(tile_of(dst, i, s.n), x_out[:, s.n % 2]).then_inc(stored[s.n % 2], 16)
                    for kind, done in (("finish", stored), ("load_x1", x1_loaded), ("load", x_loaded)):
                        for k, semaphore in enumerate(done):
                            n = sum(s.kind == kind and s.n % len(done) == k for s in steps)
                            if n:
                                sp.wait_ge(semaphore, 16 * n)

                @block.tensor
                def _(pe):
                    for s in steps:
                        n, t = s.n, s.n % T
                        if s.kind in SMALL_USES and s.use:
                            pe.wait_ge(small_taken, s.use)
                        if s.kind in OUT_USES and s.use:
                            pe.wait_ge(out_taken, s.use)
                        if s.kind in TURN_USES and s.use:
                            pe.wait_ge(turn_taken, s.use)
                        if s.kind == "h_transpose":
                            if n in loaded:
                                pe.wait_ge(x_loaded[n % T], loaded[n])
                            for k in range(KC):
                                ins = pe.transpose(small_bank[:, k * P:(k + 1) * P], x[:, n % T, k * P:(k + 1) * P], ident[:])
                            ins.then_inc(small_filled, 1)
                        if s.kind in ("project_q", "project_k", "project_v"):
                            part = ("project_q", "project_k", "project_v").index(s.kind)
                            after(pe, h_hi, "h_transpose", n, per=2)
                            after(pe, h_lo, "h_transpose", n)
                            if part < 2:
                                after(pe, by_cos_done, "rope", n - 1)
                                after(pe, by_sin_done, "rope", n - 1, per=2)
                            out = out_bank if part == 2 else qk_banks[:, part, :]
                            for k in range(KC):
                                left = [h_t[e][:, n % 2, k, 1 - k:1 - k + P] for e in range(2)]
                                right = [wqkv_t[e][:, k, part * INNER:(part + 1) * INNER] for e in range(2)]
                                ins = three(pe, out, left, right, k == 0, k == KC - 1)
                            ins.then_inc((q_ready, k_ready, out_filled)[part], 1)
                        if s.kind in ("turn_q", "turn_k"):
                            after(pe, rotated, "rope", n)
                            for k in range(OC):
                                at = (s.kind == "turn_k") * INNER + k * P
                                ins = pe.transpose(turn_bank[:, k * P:(k + 1) * P], rot[:, at:at + P], ident[:])
                            ins.then_inc(turn_filled, 1)
                        if s.kind == "window_scores":
                            after_use(pe, turn_taken, "turn_k", n)
                            if s.pair >= 2:
                                pe.wait_ge(*pair_uses[s.pair - 2])
                            bank = pair_banks[s.pair % 2]
                            pe.matmul(bank, ident_b[:], mask[:, int(t == 0)].rearrange("p h k -> p (h k)"),
                                      start=True, stop=False, skip_group_check=True)
                            for h in range(2):
                                rows, chunk = place(s.part, h)
                                for w in windows(t):
                                    at = (2 * h + w) * P
                                    ins = pe.matmul(bank[:, at:at + P], q_t[rows, chunk, :],
                                                    k_t[rows, (n - 1 + w) % 4, chunk, :], start=False,
                                                    stop=(h == 1 and w == 1), skip_group_check=True)
                            ins.then_inc(pair_filled, 1)
                        if s.kind == "p_transpose":
                            after(pe, probs_scaled, "scale", n, s.part, per=2)
                            for h in range(2):
                                for w in windows(t):
                                    at = (2 * h + w) * P
                                    ins = pe.transpose(turn_bank[:, at:at + P],
                                                       probs[:, 2 * s.part + h, w * P:(w + 1) * P], ident[:])
                            ins.then_inc(turn_filled, 1)
                        if s.kind == "attend":
                            after_use(pe, turn_taken, "p_transpose", n, s.part)
                            if s.part == 0:
                                after(pe, o_lo, "o_split", n - 1)
                            for h in range(2):
                                rows, chunk = place(s.part, h)
                                for w in windows(t):
                                    ins = pe.matmul(attend_bank[rows, chunk * P:(chunk + 1) * P],
                                                    v[:, (n - 1 + w) % 4, chunk * P + rows.start:chunk * P + rows.stop],
                                                    probs_t[:, s.part % 2, 2 * h + w, :],
                                                    start=(w == windows(t)[0]), stop=(w == 1))
                            ins.then_inc(attend_done, 1)
                        if s.kind == "wo":
                            after(pe, o_lo, "o_split", n)
                            for k in range(OC):
                                ins = three(pe, out_bank[:, 0:D], [o_t[e][:, k, :] for e in range(2)],
                                            [wo_t[e][:, k, :] for e in range(2)], k == 0, k == OC - 1)
                            ins.then_inc(out_filled, 1)
                        if s.kind == "y_transpose":
                            after_use(pe, out_taken, "wo", n)
                            pe.transpose(small_bank[:, 0:P], y[:, n % BODY, P:D], ident[:]).then_inc(small_filled, 1)
                        if s.kind == "y_shift":
                            after(pe, y_t_done, "y_transpose", n)
                            after_use(pe, small_taken, "y_transpose", n)
                            pe.transpose(small_bank[:, 0:P], y_t[:, n % 2, 0:P], ident[:]).then_inc(small_filled, 1)
                        if s.kind == "ln_transpose":
                            after(pe, y_normed, "ln_apply", n, per=2)
                            for k in range(KC):
                                ins = pe.transpose(small_bank[:, k * P:(k + 1) * P], normed[:, n % 2, k * P:(k + 1) * P],
                                                   ident[:])
                            ins.then_inc(small_filled, 1)
                        if s.kind == "mlp_in":
                            after(pe, ln_lo, "ln_transpose", n + MGRP - 1)
                            width = min(HCW, HID - s.part * HCW)
                            for half in range(2):
                                if s.pair + half >= 2:
                                    pe.wait_ge(*pair_uses[s.pair + half - 2])
                                cols = half * HID + s.part * HCW
                                out = pair_banks[(s.pair + half) % 2][0:width, :]
                                for k in range(KC):
                                    ins = three(pe, out, [w1_t[e][:, k, cols:cols + width] for e in range(2)],
                                                [ln_t[e][:, n // MGRP % 2, k, :] for e in range(2)], k == 0, k == KC - 1)
                                ins.then_inc(pair_filled, 1)
                        if s.kind == "mlp_out":
                            after(pe, hid_lo, "mlp_in", n // MGRP * MGRP, HCH - 1)
                            for k in range(HCH):
                                width = min(HCW, HID - k * HCW)
                                cols = slice(n % MGRP * P, (n % MGRP + 1) * P)
                                ins = three(pe, out_bank[:, 0:D], [hid[e][0:width, k, cols] for e in range(2)],
                                            [w2_t[e][0:width, k, :] for e in range(2)], k == 0, k == HCH - 1)
                            ins.then_inc(out_filled, 1)

                @block.scalar
                def _(act):
                    for s in steps:
                        n, t = s.n, s.n % T
                        if s.kind == "h_transpose":
                            act.wait_ge(small_filled, s.use + 1)
                            act.copy(h_t[0][:, n % 2, :, 1:P + 1], small_bank[:, 0:D].rearrange("p (k q) -> p k q", k=KC))\
                               .then_inc(h_hi, 1)
                            before = h_t[0][:, (n - 1) % 2, 1, P:P + 1].bitcast(F32) if t else zero_col[:]
                            after(act, h_hi, "h_transpose", n - 1, per=2)
                            act.copy(h_t[0][:, n % 2, 1, 0:1], before).then_inc(h_hi, 1)
                        if s.kind == "project_v":
                            act.wait_ge(out_filled, s.use + 1)
                            act.copy(v[:, n % 4, :], out_bank).then_inc(out_taken, 1)
                        if s.kind == "rope":
                            act.wait_ge(q_ready, s.count)
                            act.wait_ge(k_ready, s.count)
                            after(act, rotated, "rope", n - 1)
                            act.square(work_a.rearrange("p w h d -> p (w h d)"),
                                       qk_banks.rearrange("p w c -> p (w c)")).then_inc(squared, 1)
                        if s.kind in ("turn_q", "turn_k"):
                            act.wait_ge(turn_filled, s.use + 1)
                            out = q_t[:] if s.kind == "turn_q" else k_t[:, n % 4]
                            act.copy(out, turn_bank.rearrange("p (k q) -> p k q", k=OC)).then_inc(turn_taken, 1)
                        if s.kind == "p_transpose" and s.part % 2:
                            take_probs(act, act.copy, s)
                        if s.kind == "window_scores":
                            act.wait_ge(max_done, s.count)
                            bank = pair_banks[s.pair % 2]
                            for h in range(2):
                                head = 2 * s.part + h
                                act.activation(probs[:, head, :], bank[:, 2 * h * P:2 * (h + 1) * P], ACT.Exp,
                                               bias=neg_max[:, n % 2, head:head + 1],
                                               accum_out=sums[:, n % 2, head:head + 1]).then_inc(exp_done, 1)
                        if s.kind == "scale":
                            act.wait_ge(sums_inverted, s.count)
                            for h in range(2):
                                head = 2 * s.part + h
                                act.activation(probs[:, head, :], probs[:, head, :], ACT.Copy,
                                               scale=inv_sums[:, n % 2, head:head + 1]).then_inc(probs_scaled, 1)
                        if s.kind == "o_split":
                            after(act, attend_done, "attend", n, 3)
                            act.copy(o_t[0][:], attend_bank.rearrange("p (k q) -> p k q", k=OC)).then_inc(o_hi, 1)
                        if s.kind == "y_transpose":
                            act.wait_ge(small_filled, s.use + 1)
                            before = y_t[:, (n - 1) % 2, P:P + 1] if t else zero_col[:]
                            after_use(act, small_taken, "y_transpose", n - 1)
                            act.copy(y_t[:, n % 2, 0:1], before).then_inc(y_t_done, 1)
                            act.copy(y_t[:, n % 2, 1:P + 1], small_bank[:, 0:P]).then_inc(small_taken, 1)
                        if s.kind == "y_shift":
                            act.wait_ge(small_filled, s.use + 1)
                            act.copy(normed[:, n % 2, P:D], small_bank[:, 0:P]).then_inc(small_taken, 1)
                        if s.kind == "ln_transpose":
                            act.wait_ge(small_filled, s.use + 1)
                            if s.count > 1:
                                act.wait_ge(ln_lo, s.count - 1)
                            for k, done in enumerate((shifted, small_taken)):
                                act.activation(ln_full[:, k, :], small_bank[:, k * P:(k + 1) * P], ACT.Identity,
                                               scale=gain[:, k:k + 1], bias=shift[:, k:k + 1]).then_inc(done, 1)
                        if s.kind == "mlp_in":
                            act.wait_ge(pair_filled, s.pair + 2)
                            if s.count > 1:
                                act.wait_ge(hid_product, s.count - 1)
                            width = min(HCW, HID - s.part * HCW)
                            act.activation(gate[0:width, :], pair_banks[(s.pair + 1) % 2][0:width, :], ACT.Gelu,
                                           bias=b1_g[0:width, s.part:s.part + 1]).then_inc(gated, 1)

                @block.vector
                def _(dve):
                    for s in steps:
                        n, t = s.n, s.n % T
                        if s.kind == "h_transpose":
                            dve.wait_ge(h_hi, 2 * s.count - 1)
                            dve.tensor_tensor(h_t[1][:, n % 2, :, 1:P + 1], small_bank[:, 0:D].rearrange("p (k q) -> p k q", k=KC),
                                              h_t[0][:, n % 2, :, 1:P + 1].bitcast(F32), ALU.subtract).then_inc(small_taken, 1)
                            before = h_t[1][:, (n - 1) % 2, 1, P:P + 1].bitcast(F32) if t else zero_col[:]
                            after_use(dve, small_taken, "h_transpose", n - 1)
                            dve.tensor_copy(h_t[1][:, n % 2, 1, 0:1], before).then_inc(h_lo, 1)
                        if s.kind == "rope":
                            dve.wait_ge(squared, s.count)
                            dve.tensor_reduce(squares_sum[:, n % 2, :], work_a.rearrange("p w h d -> p (w h) d"), AX.X, ALU.add)\
                               .then_inc(squares_summed, 1)
                            if s.count > 1:
                                dve.wait_ge(rope_added, s.count - 1)
                            qk = qk_banks.rearrange("p w (h d) -> p w h d", h=H2)
                            table = rope_s[:, t].unsqueeze(2).to_broadcast([P, 2, H2, HD2])
                            for e in range(2):
                                to, of = slice(32 * e, 32 * e + 32), slice(32 - 32 * e, 64 - 32 * e)
                                dve.tensor_tensor(work_b[:, :, :, to], qk[:, :, :, of], table[:, :, :, to], ALU.mult)\
                                   .then_inc(by_sin_done, 1)
                            table = rope_c[:, t].unsqueeze(2).to_broadcast([P, 2, H2, HD2])
                            dve.wait_ge(squares_summed, s.count)
                            dve.tensor_tensor(work_a[:], qk, table, ALU.mult).then_inc(by_cos_done, 1)
                        if s.kind == "p_transpose" and s.part % 2 == 0:
                            take_probs(dve, dve.tensor_copy, s)
                        if s.kind == "window_scores":
                            dve.wait_ge(pair_filled, s.pair + 1)
                            dve.tensor_reduce(neg_max[:, n % 2, 2 * s.part:2 * s.part + 2],
                                              pair_banks[s.pair % 2].rearrange("p (h k) -> p h k", h=2), AX.X, ALU.max,
                                              negate=True).then_inc(max_done, 1)
                        if s.kind == "scale":
                            after(dve, exp_done, "window_scores", n, s.part, per=2)
                            heads = slice(2 * s.part, 2 * s.part + 2)
                            dve.reciprocal(inv_sums[:, n % 2, heads], sums[:, n % 2, heads]).then_inc(sums_inverted, 1)
                        if s.kind == "o_split":
                            dve.wait_ge(o_hi, s.count)
                            dve.tensor_tensor(o_t[1][:], attend_bank.rearrange("p (k q) -> p k q", k=OC),
                                              o_t[0][:].bitcast(F32), ALU.subtract).then_inc(o_lo, 1)
                        if s.kind == "wo":
                            dve.wait_ge(out_filled, s.use + 1)
                            if n in loaded:
                                dve.wait_ge(x_loaded[n % T], loaded[n])
                            dve.tensor_tensor(y[:, n % BODY, :], out_bank[:, 0:D], x[:, n % T, :], ALU.add).then_inc(out_taken, 1)
                        if s.kind == "y_shift":
                            after_use(dve, out_taken, "wo", n)
                            dve.bn_stats(stats[:, n % 2, 0, :], y[:, n % BODY, 0:P]).then_inc(y_stats, 1)
                            dve.wait_ge(small_taken, s.use + 1)
                            dve.bn_stats(stats[:, n % 2, 1, :], normed[:, n % 2, P:D]).then_inc(y_stats, 1)
                            dve.wait_ge(y_stats, 2 * s.count)
                            if s.count > 1:
                                dve.wait_ge(y_eps, s.count - 1)
                            dve.bn_aggr(mean_var[:, n % 2], stats[:, n % 2].rearrange("p a b -> p (a b)")).then_inc(y_mean, 1)
                        if s.kind == "ln_apply":
                            after(dve, y_rstd, "y_shift", n)
                            for k, src in enumerate((y[:, n % BODY, 0:P], normed[:, n % 2, P:D])):
                                dve.tensor_scalar(normed[:, n % 2, k * P:(k + 1) * P], src, mean_var[:, n % 2, 0:1],
                                                  rstd[:, n % 2], ALU.subtract, ALU.mult).then_inc(y_normed, 1)
                        if s.kind == "ln_transpose":
                            dve.wait_ge(shifted, s.count)
                            dve.wait_ge(small_taken, s.use + 1)
                            at = slice(n % MGRP * P, (n % MGRP + 1) * P)
                            hi, lo = (ln_t[e][:, n // MGRP % 2, :, at] for e in range(2))
                            dve.tensor_copy(hi, ln_full[:]).then_inc(ln_hi, 1)
                            dve.wait_ge(ln_hi, s.count)
                            dve.tensor_tensor(lo, ln_full[:], hi.bitcast(F32), ALU.subtract).then_inc(ln_lo, 1)
                        if s.kind == "mlp_in":
                            width = min(HCW, HID - s.part * HCW)
                            dve.wait_ge(gated, s.count)
                            if s.count > 1:
                                dve.wait_ge(hid_lo, s.count - 1)
                            dve.scalar_tensor_tensor(hid_full[0:width, :], pair_banks[s.pair % 2][0:width, :],
                                                     b1_a[0:width, s.part:s.part + 1], gate[0:width, :], ALU.add, ALU.mult)\
                               .then_inc(hid_product, 1)
                            hi, lo = (hid[e][0:width, s.part, :] for e in range(2))
                            dve.wait_ge(hid_product, s.count)
                            dve.tensor_copy(hi, hid_full[0:width, :]).then_inc(hid_hi, 1)
                            dve.wait_ge(hid_hi, s.count)
                            dve.tensor_tensor(lo, hid_full[0:width, :], hi.bitcast(F32), ALU.subtract).then_inc(hid_lo, 1)
                        if s.kind == "mlp_out":
                            dve.wait_ge(out_filled, s.use + 1)
                            after(dve, y_biased, "ln_apply", n)
                            if ("finish", n - 2, 0) in made:
                                dve.wait_ge(stored[n % 2], 16 * sum(k[0] == "finish" and k[1] % 2 == n % 2 and
                                                                    made[k] <= made["finish", n - 2, 0] for k in made))
                            dve.tensor_tensor(x_out[:, n % 2], out_bank[:, 0:D], y[:, n % BODY, :], ALU.add)\
                               .then_inc(out_taken, 1)
                            if last:
                                dve.wait_ge(out_taken, s.use + 1)
                                if ("load_x1", n, 0) in made:
                                    dve.wait_ge(x1_loaded[n % 2], 16 * sum(k[0] == "load_x1" and k[1] % 2 == n % 2 and
                                                                           made[k] <= made["load_x1", n, 0] for k in made))
                                dve.tensor_tensor(x_out[:, n % 2], x_out[:, n % 2], x1_in[:, n % 2], ALU.add)\
                                   .then_inc(f_summed, 1)
                        if s.kind == "finish_mean" and last:
                            after(dve, f_summed, "mlp_out", n)
                            dve.bn_stats(f_stats[:, n % 2], x_out[:, n % 2]).then_inc(f_stats_done, 1)
                            dve.wait_ge(f_stats_done, s.count)
                            if s.count > 2:
                                dve.wait_ge(f_eps, s.count - 2)
                            dve.bn_aggr(f_mean_var[:, n % 2], f_stats[:, n % 2]).then_inc(f_mean, 1)
                        if s.kind == "finish" and last:
                            after(dve, f_rstd_done, "finish_mean", n)
                            dve.tensor_scalar(x_out[:, n % 2], x_out[:, n % 2], f_mean_var[:, n % 2, 0:1],
                                              f_rstd[:, n % 2], ALU.subtract, ALU.mult).then_inc(x_out_ready, 1)

                @block.gpsimd
                def _(pool):
                    def inverse_root(of, plus_eps, out, eps_done, root_done, count):
                        pool.tensor_scalar(plus_eps, of, LN_EPS, None, ALU.add).then_inc(eps_done, 1)
                        pool.wait_ge(eps_done, count)
                        pool.tensor_tensor(out, plus_eps, exponent[:, 0:1], ALU.pow).then_inc(root_done, 1)

                    for s in steps:
                        n = s.n
                        if s.kind == "rope":
                            pool.wait_ge(squares_summed, s.count)
                            pool.tensor_scalar(clipped[:, n % 2], squares_sum[:, n % 2], 1e-24, None, ALU.max)\
                                .then_inc(norms_clipped, 1)
                            pool.wait_ge(norms_clipped, s.count)
                            pool.tensor_tensor(inv_norm[:, n % 2], clipped[:, n % 2], exponent[:], ALU.pow)\
                                .then_inc(norms_ready, 1)
                            pool.wait_ge(by_cos_done, s.count)
                            pool.wait_ge(by_sin_done, 2 * s.count)
                            pool.tensor_tensor(work_a[:], work_a[:], work_b[:], ALU.add).then_inc(rope_added, 1)
                            pool.wait_ge(rope_added, s.count)
                            pool.wait_ge(norms_ready, s.count)
                            after_use(pool, turn_filled, "turn_k", n - 1)
                            pool.tensor_tensor(rot.rearrange("p (g d) -> p g d", d=HD2),
                                               work_a.rearrange("p w h d -> p (w h) d"),
                                               inv_norm[:, n % 2].unsqueeze(2).to_broadcast([P, 2 * H2, HD2]), ALU.mult)\
                                .then_inc(rotated, 1)
                        if s.kind == "y_shift":
                            pool.wait_ge(y_mean, s.count)
                            inverse_root(mean_var[:, n % 2, 1:2], var_eps[:, n % 2], rstd[:, n % 2], y_eps, y_rstd, s.count)
                        if s.kind == "ln_apply":
                            pool.wait_ge(y_normed, 2 * s.count)
                            pool.tensor_tensor(y[:, n % BODY, :], y[:, n % BODY, :], b2_all[:], ALU.add).then_inc(y_biased, 1)
                        if s.kind == "finish_mean" and last:
                            pool.wait_ge(f_mean, s.count)
                            inverse_root(f_mean_var[:, n % 2, 1:2], f_var_eps[:, n % 2], f_rstd[:, n % 2], f_eps, f_rstd_done,
                                         s.count)

            nc.all_engine_barrier(sems_to_clear=range(min(sem_nums), max(sem_nums) + 1))

        sem_nums = [s.num for s in sems]

        pieces = []

        def piece(src, terms_of, rows=P):
            pieces.append((src, terms_of, rows))

        for k in range(KC):
            for w, total, src in ((wqkv_t, 3 * INNER, wqkv), (w1_t, 2 * HID, w1)):
                for c in range(0, total, 2 * INNER):
                    cols = slice(c, min(c + 2 * INNER, total))
                    piece(src[layer, k * P:(k + 1) * P, cols], [w[e][:, k, cols] for e in range(2)])
        piece(wo[layer].rearrange("(k p) n -> p k n", p=P), [wo_t[e][:] for e in range(2)])
        for a, b in ((0, 3), (3, HCH - 1)):
            piece(w2[layer, a * HCW:b * HCW, :].rearrange("(k p) n -> p k n", p=HCW),
                  [w2_t[e][:, a:b, :] for e in range(2)], HCW)
        tail = HID - (HCH - 1) * HCW
        piece(w2[layer, (HCH - 1) * HCW:HID, :], [w2_t[e][0:tail, HCH - 1, :] for e in range(2)], tail)
        staging = [work_a.rearrange("p w h d -> p (w h d)"), work_b.rearrange("p w h d -> p (w h d)")]

        def staged(k):
            src, out, rows = pieces[k]
            tile = staging[k % 2][0:rows, 0:int(np.prod(out[0].shape[1:]))]
            return tile if len(out[0].shape) == 2 else tile.rearrange("p (a b) -> p a b", a=out[0].shape[1])

        with nc.Block() as block:
            @block.sync
            def _(sp):
                for k, (src, _, _) in enumerate(pieces):
                    if k >= 2:
                        sp.wait_ge(stage_lo, k - 1)
                    sp.dma_start(staged(k), src).then_inc(stage_loaded[k % 2], 16)

            constants = [
                (rot[:], mask_in.rearrange("q f h k -> q (f h k)")), (ident[:], ident_in),
                (rope_c[:], tables[0].rearrange("(t p) w d -> p t w d", p=P)),
                (rope_s[:], tables[1].rearrange("(t p) w d -> p t w d", p=P)),
                (gain[:], ln_g[layer].rearrange("(k p) -> p k", p=P)),
                (shift[:], ln_b[layer].rearrange("(k p) -> p k", p=P)),
                (b2_all[:], b2[layer].partition_broadcast(P)),
                (scales[:, 0], q_scale[layer].partition_broadcast(P)),
                (scales[:, 1], k_scale[layer].partition_broadcast(P)),
            ]
            for half, to in enumerate((b1_a, b1_g)):
                full = (HCH - 1) * HCW
                constants.append((to[:, 0:HCH - 1], b1[layer, half * HID:half * HID + full].rearrange("(k p) -> p k", p=HCW)))
                constants.append((to[0:tail, HCH - 1:HCH],
                                  b1[layer, half * HID + full:(half + 1) * HID].rearrange("(p k) -> p k", k=1)))

            @block.scalar
            def _(act):
                for out, src in constants:
                    act.dma_start(out, src, allow_slow_non_contiguous=True).then_inc(constants_loaded, 16)
                act.wait_ge(constants_loaded, 16 * len(constants))

            @block.gpsimd
            def _(pool):
                pool.memset(exponent[:], -0.5)
                pool.memset(zero_col[:], 0.0)

            @block.vector
            def _(dve):
                for k, (_, out, _) in enumerate(pieces):
                    dve.wait_ge(stage_loaded[k % 2], 16 * (k // 2 + 1))
                    dve.tensor_copy(out[0], staged(k)).then_inc(stage_hi, 1)
                    dve.wait_ge(stage_hi, k + 1)
                    dve.tensor_tensor(out[1], staged(k), out[0].bitcast(F32), ALU.subtract).then_inc(stage_lo, 1)
                dve.wait_ge(constants_loaded, 16 * len(constants))
                dve.tensor_copy(ident_b[:], ident[:])
                dve.tensor_copy(mask.rearrange("p f h k -> p (f h k)"), rot[:])
                for w in range(2):
                    dve.tensor_tensor(rope_c[:, :, w], rope_c[:, :, w],
                                      scales[:, w].unsqueeze(1).to_broadcast([P, T, HD2]), ALU.mult)
                    for e in range(2):
                        to, of = slice(32 * e, 32 * e + 32), slice(32 - 32 * e, 64 - 32 * e)
                        dve.tensor_tensor(rope_s[:, :, w, to], rope_s[:, :, w, to],
                                          scales[:, w, of].unsqueeze(1).to_broadcast([P, T, HD2 // 2]), ALU.mult)
        nc.all_engine_barrier(sems_to_clear=range(min(sem_nums), max(sem_nums) + 1))
        section("first", 0)
        with nc.Fori(1, B * T // BODY) as i:
            section("body", i)
        section("last", B * T // BODY)


def rope_tables():
    exponents = -np.arange(0, HD1, 2).astype(np.float32) / np.float32(HD1)
    angles = np.arange(S, dtype=np.float32)[:, None] * (np.float32(10000.0) ** exponents)[None, :]
    cos, sin = np.cos(angles), np.sin(angles)
    return np.repeat(cos, 2, axis=1), np.stack([-sin, sin], -1).reshape(S, HD1)


def xpos_tables():
    f32 = np.float32
    half = np.arange(0, HD2, 2, dtype=f32)
    t = np.arange(S, dtype=f32)
    angles = t[:, None] * (f32(1.0) / f32(10000.0) ** (half / f32(HD2)))[None, :]
    scale = ((half + f32(0.4 * HD2)) / f32(1.4 * HD2))[None, :] ** ((t - S // 2) / f32(WINDOW // 2))[:, None]
    cos, sin = np.cos(angles), np.sin(angles)
    cos, scale = np.concatenate([cos, cos], -1), np.concatenate([scale, scale], -1)
    sin = np.concatenate([-sin, sin], -1)
    grow, fall = scale * f32(QK_SCALE), f32(1.0) / scale
    return (np.stack([cos * grow, cos * fall], 1).astype(f32), np.stack([sin * grow, sin * fall], 1).astype(f32))


def window_mask():
    i, j = np.arange(P)[:, None], np.arange(2 * WINDOW)[None, :]
    outside = (j < i) | (j > i + WINDOW)
    outside = np.stack([outside, outside | (j < WINDOW)], 1)
    return np.repeat(np.where(outside, np.float32(MASKED), np.float32(0.0))[:, :, None, :], 2, axis=2)


LAYER_INS = ("wqkv", "q_scale", "k_scale", "wo", "ln_g", "ln_b", "w1", "b1", "w2", "b2")


def kernel(**inputs):
    import concourse.bacc as bacc
    from concourse.bass_utils import run_bass_kernel_spmd

    nc = bacc.Bacc("TRN2", target_bir_lowering=False, num_devices=1)
    arrays = {}

    def given(name, a):
        arrays[name] = np.ascontiguousarray(a)
        return nc.dram_tensor(name, arrays[name].shape, mybir.dt.from_np(arrays[name].dtype), kind="ExternalInput").ap()

    first = {k: inputs["L0_attn_" + k] for k in ("x", "Wq", "bq", "Wk", "bk", "Wv", "bv", "Wo")}
    cos, sin = rope_tables()
    xpos_cos, xpos_sin = xpos_tables()
    ident = given("ident", np.eye(P, dtype=np.float32))
    x1 = nc.dram_tensor("x1_scratch", (B + 1, S, D), F32, kind="Internal").ap()
    x2 = nc.dram_tensor("x2_scratch", (B, S, D), F32, kind="Internal").ap()
    out = nc.dram_tensor("out", (B, S, D), F32, kind="ExternalOutput").ap()

    attention_pass(nc, given("x", first["x"]),
                   given("wqkv_t", np.concatenate([first["Wq"], first["Wk"], first["Wv"]]).T),
                   given("bqkv", np.concatenate([first["bq"], first["bk"], first["bv"]])),
                   given("wo_t", np.asarray(first["Wo"]).T),
                   given("rope_cos", cos), given("rope_sin", sin), ident, x1)
    weights = [given("layers_" + name, inputs["L0_ffn_" + name]) for name in LAYER_INS]
    tables = given("xpos_cos", xpos_cos), given("xpos_sin", xpos_sin)
    mask = given("window_mask", window_mask())
    layer_pass(nc, 0, False, x1[1:], None, x2, *weights, tables, mask, ident)
    layer_pass(nc, 1, True, x2, x1[1:], out, *weights, tables, mask, ident)

    result = run_bass_kernel_spmd(nc, [arrays], core_ids=[0])
    return result.results[0]["out"]
```

```python
from contextlib import ExitStack

import numpy as np
import concourse.bass as bass
from concourse import mybir

F32 = mybir.dt.float32
F32R = mybir.dt.float32r
BF16 = mybir.dt.bfloat16
ALU = mybir.AluOpType
ACT = mybir.ActivationFunctionType
AX = mybir.AxisListType

P = 128
B, S, D = 8, 1024, 256
T = S // P
KC = D // P
HALF = 512
LN_EPS = 1e-5

H1 = 16
HD1 = D // H1
GRP = 4
G = H1 // GRP
TERMS = 6
STACK = TERMS * HD1
MAXR = 2
VW = HD1 + 1
TH = T // 2
CYC = 2 * T
INV_SCALE = 1.0 / np.sqrt(float(D))


class Step:

    def __init__(self, kind, n=0, part=0, m=0, misc_now=0, t=0, par=0, g=0, slot=0, u=0, c=0, j=0, half=0, batch=0,
                 first=False):
        self.kind, self.n, self.part = kind, n, part
        self.m, self.misc_now = m, misc_now
        self.t, self.par, self.g, self.slot = t, par, g, slot
        self.u, self.c, self.j, self.half = u, c, j, half
        self.batch, self.first = batch, first


def plan_attention(section):
    steps, count = [], {}

    def add(kind, misc=False, **at):
        at["n"] = count.get(kind, 0)
        count[kind] = at["n"] + 1
        if misc:
            at["m"] = count.get("misc", 0)
            count["misc"] = at["m"] + 1
        at["misc_now"] = count.get("misc", 0)
        steps.append(Step(kind, **at))

    def project(t, par, part):
        if part == 0:
            add("x_transpose", True, t=t)
        if part == 1:
            add("qk_project", True, t=t, par=par)
        if part == 2:
            add("v_project", True, t=t, par=par)
            if section == "prologue":
                rope(t, par)

    def rope(t, par):
        for kind in ("rope_cos", "rope_sin", "rope"):
            add(kind, t=t, par=par)

    def maxima(k, slot):
        half = k // (GRP * T // 2)
        add("row_max", slot=slot, j=k // TH % GRP, t=half * TH + k % TH)

    def move_maxima(part, half, slot):
        if part in (0, 1):
            add(("max_hi", "max_lo")[part], half=half, m=count.get("row_max", 0))
        if part == 3:
            add("max_rows", True, slot=slot, half=half)

    if section == "prologue":
        add("load_x", batch=0, first=True)
        for t in range(T + 1):
            for part in range(2):
                if t < T:
                    project(t, 0, part)
            for kind in ("split_1", "rest_1", "split_2", "split_3"):
                if t:
                    add(kind, t=t - 1, par=0, g=0)
            if t < T:
                project(t, 0, 2)
            if t:
                add("stack", True, t=t - 1, slot=0)
        add("load_x", batch=1, first=False)
        for k in range(GRP * T):
            maxima(k, 0)
            for kind in (("split_1", "rest_1"), ("split_2", "split_3"), (), ())[k % GRP]:
                add(kind, t=k // GRP, par=0, g=1)
            if k % GRP == 3:
                add("stack", True, t=k // GRP, slot=1)
            if k == GRP * TH - 1:
                for part in (0, 1, 3):
                    move_maxima(part, 0, 0)
    if section == "body":
        for u in range(2 * G):
            par, g = u // G, u % G
            nxt = (u + 2) // G % 2, (u + 2) % G
            done = 0
            for c in range(CYC):
                if c == 0 and u in (2, 6):
                    add("load_x", batch=u // 2 + 1 if u == 2 else 3, first=False)
                if c == 0 and u in (1, 5):
                    add("load_residual", par=par, first=(u == 1))
                for j in range(GRP):
                    add("scores", u=u, c=c, j=j, slot=g)
                    if done < min(GRP * T, -(-T * (GRP * c + j + 1) // CYC)):
                        maxima(done, (u + 1) % G)
                        done += 1
                    if c % 2 == 0:
                        add(("split_1", "rest_1", "split_2", "split_3")[j], t=c // 2, par=nxt[0], g=nxt[1])
                    if j == 0 and c in (3, 7):
                        add("divide", True, half=c // 4, u=(u - 1) % 2, par=(u - 1) // G % 2, g=(u - 1) % G)
                        add("divide_apply", half=c // 4, u=(u - 1) % 2, par=(u - 1) // G % 2, g=(u - 1) % G)
                    if j == 3 and c % 2 == 1:
                        add("stack", True, t=c // 2, slot=nxt[1])
                    if j == 1 and g < 2 and c % 4 < 2:
                        project(4 * g + c // 4, 1 - par, c % 4)
                    if j == 1 and g >= 2 and c % 4 == 1:
                        add("out_transpose", True, t=4 * (g - 2) + c // 4, par=1 - par)
                    if j == 2 and g >= 2 and c % 4 == 2:
                        add("out_project", True, t=4 * (g - 2) + c // 4, par=1 - par)
                    if g >= 2 and c % 4 == 2 and j > 1:
                        add(("norm_stats", "norm_mean")[j - 2])
                    if (c, j) in ((T, 2), (T, 3), (T + 1, 2)):
                        move_maxima(j - 2 if c == T else 3, 0, (u + 1) % G)
                    if (c, j) in ((0, 2), (0, 3), (1, 2)):
                        move_maxima(j - 2 if c == 0 else 3, 1, g)
                    if j == 2 and g < 2 and c % 4 == 2:
                        project(4 * g + c // 4, 1 - par, 2)
                    if g < 2 and (c % 4, j) in ((2, 3), (3, 1), (3, 3)):
                        add(("rope_cos", "rope_sin", "rope")[(c % 4 - 2) + (j == 3) * (c % 4 - 2)],
                            t=4 * g + c // 4, par=1 - par)
                if c:
                    add("values", u=u, c=c - 1, par=par, g=g)
                elif u:
                    add("values", u=u - 1, c=CYC - 1, par=(u - 1) // G, g=(u - 1) % G)
                if g >= 2 and c % 4 == 3:
                    add("norm_apply", t=4 * (g - 2) + c // 4, par=1 - par)
        add("values", u=2 * G - 1, c=CYC - 1, par=1, g=G - 1)
    if section == "epilogue":
        for half in range(2):
            add("divide", True, half=half, u=1, par=1, g=G - 1)
            add("divide_apply", half=half, u=1, par=1, g=G - 1)
        for t in range(T):
            add("out_transpose", True, t=t, par=1)
            add("out_project", True, t=t, par=1)
            add("norm_stats")
            add("norm_mean")
            add("norm_apply", t=t, par=1)
    return steps


def attention_pass(nc, x, wqkv_t, bqkv, wo_t, rope_cos, rope_sin, ident_in, x1_scratch):
    with ExitStack() as ctx:
        def sb(name, shape, dt=F32):
            return ctx.enter_context(nc.sbuf_tensor(name, shape, dt))

        sems = []

        def sem(name):
            s = ctx.enter_context(nc.semaphore(name))
            sems.append(s)
            return s

        psum = ctx.enter_context(nc.psum_tensor("a_psum", [P, 8, HALF], F32))
        max_banks = [psum[:, 0:2, :], psum[:, 2:4, :]]
        score_banks = [psum[:, 4, :], psum[:, 5, :]]
        value_bank = psum[:, 6, :]
        misc_bank = psum[:, 7, :]
        misc_half = misc_bank.bitcast(BF16)

        w_qkv = sb("a_wqkv", [P, KC, 3 * D])
        w_out = sb("a_wo", [P, KC, D])
        bias = sb("a_bias", [P, 3 * D])
        ident = sb("a_ident", [P, P])
        cos_t = sb("a_cos", [P, T, HD1])
        sin_t = sb("a_sin", [P, T, HD1])
        x_in = sb("a_x_in", [P, T, D])
        x_res = sb("a_x_res", [P, 2, T, D])
        x_tr = sb("a_x_tr", [P, KC, P])
        qk = sb("a_qk", [P, 2 * D])
        by_cos = sb("a_by_cos", [P, 2 * D])
        by_sin = sb("a_by_sin", [P, 2 * D])
        rest = sb("a_rest", [P, 2, GRP, HD1])
        roped = sb("a_roped", [P, 2, T, 2 * D])
        v_ones = sb("a_v_ones", [P, 2, T, H1, VW])
        source = sb("a_source", [P, 2, 2, GRP, P], BF16)
        stacks = sb("a_stacks", [P, G, 2, GRP, S], BF16)
        row_max = sb("a_row_max", [P, GRP, T])
        max_terms = sb("a_max_terms", [P, GRP, MAXR, TH], BF16)
        max_row = sb("a_max_row", [GRP * MAXR * TH, P], BF16)
        ident_b = sb("a_ident_b", [P, P], BF16)
        probs = sb("a_probs", [P, 2 * GRP, HALF])
        values_tr = sb("a_values_tr", [P, 2, S])
        recip = sb("a_recip", [P, 2, 4, GRP])
        attn = sb("a_attn", [P, 2, T, D])
        attn_tr = sb("a_attn_tr", [P, KC, P])
        res = sb("a_res", [P, 2, D])
        stats = sb("a_stats", [P, 2, 6])
        mean_var = sb("a_mean_var", [P, 2, 2])
        var_eps = sb("a_var_eps", [P, 2, 1])
        rstd = sb("a_rstd", [P, 2, 1])
        minus_half = sb("a_minus_half", [P, 1])
        x1_out = sb("a_x1_out", [P, 2, D])

        constants_loaded = sem("a_constants_loaded")
        preset = sem("a_preset")
        x_loaded = sem("a_x_loaded")
        residual_loaded = sem("a_residual_loaded")
        misc_filled = sem("a_misc_filled")
        misc_taken = sem("a_misc_taken")
        cos_done = sem("a_cos_done")
        sin_done = sem("a_sin_done")
        roped_done = sem("a_roped_done")
        hi_done = sem("a_hi_done")
        lo_done = sem("a_lo_done")
        dup_done = sem("a_dup_done")
        rest_done = sem("a_rest_done")
        mid_done = sem("a_mid_done")
        max_hi = sem("a_max_hi")
        max_lo = sem("a_max_lo")
        max_scores = sem("a_max_scores")
        max_taken = sem("a_max_taken")
        max_row_stored = sem("a_max_row_stored")
        scores_ready = sem("a_scores_ready")
        probs_ready = sem("a_probs_ready")
        values_done = sem("a_values_done")
        values_copied = sem("a_values_copied")
        recip_done = sem("a_recip_done")
        stats_done = sem("a_stats_done")
        mean_done = sem("a_mean_done")
        eps_done = sem("a_eps_done")
        rstd_done = sem("a_rstd_done")
        x1_ready = sem("a_x1_ready")
        x1_stored = [sem(f"a_x1_stored_{k}") for k in range(2)]

        x_t = x.rearrange("b (t p) d -> b p t d", p=P)
        slots_t = x1_scratch.rearrange("b (t p) d -> b p t d", p=P)

        def heads(ap, n):
            return ap.rearrange("p (h d) -> p h d", h=n)

        value_sums = misc_bank.rearrange("p (k j d) -> p k j d", k=4, j=GRP)

        def terms(k):
            return source[:, k, :, :, 0:STACK].rearrange("p w j (e d) -> p w j e d", e=TERMS)

        def section(name, i=None):
            steps = plan_attention(name)
            stack_m = [s.m for s in steps if s.kind == "stack"]
            max_m = [s.m for s in steps if s.kind == "max_rows"]
            stack_ready = {}
            rows_ready = {}
            rows = 0
            for s in steps:
                if s.kind in ("row_max", "scores"):
                    s.stack_need = stack_ready.get(s.slot, 0)
                    s.rows_need = rows_ready.get((s.slot, s.c // T), 0)
                if s.kind == "stack":
                    stack_ready[s.slot] = s.m + 1
                if s.kind == "max_rows":
                    rows += 16 * GRP
                    rows_ready[s.slot, s.half] = rows

            with nc.Block() as block:
                @block.sync
                def _(sp):
                    for s in steps:
                        if s.kind == "load_x":
                            if s.misc_now and not s.first:
                                sp.wait_ge(misc_filled, s.misc_now)
                            src = x_t[s.batch] if i is None else x_t[(2 * i + s.batch) % B]
                            sp.dma_start(x_in[:], src).then_inc(x_loaded, 16)
                        if s.kind == "load_residual":
                            if not s.first:
                                sp.wait_ge(misc_taken, s.misc_now)
                            sp.dma_start(x_res[:, s.par], x_t[2 * i + s.par]).then_inc(residual_loaded, 16)
                        if s.kind == "max_rows":
                            sp.wait_ge(misc_taken, s.m + 1)
                            for j in range(GRP):
                                dst = stacks[STACK:STACK + MAXR, s.slot, 0, j, s.half * HALF:(s.half + 1) * HALF]
                                sp.dma_start(dst.rearrange("p (t q) -> p t q", t=TH),
                                             max_row[j * MAXR * TH:(j + 1) * MAXR * TH, :]).then_inc(max_row_stored, 16)
                        if s.kind == "norm_apply":
                            sp.wait_ge(x1_ready, s.n + 1)
                            slot = B if i is None else 2 * i + 1 - s.par
                            sp.dma_start(slots_t[slot][:, s.t, :], x1_out[:, s.n % 2]).then_inc(x1_stored[s.n % 2], 16)
                    stores = sum(s.kind == "norm_apply" for s in steps)
                    for k in range(2):
                        if stores:
                            sp.wait_ge(x1_stored[k], 16 * (stores // 2))
                    for kind, done in (("load_x", x_loaded), ("load_residual", residual_loaded)):
                        n = sum(s.kind == kind for s in steps)
                        if n:
                            sp.wait_ge(done, 16 * n)
                    if rows:
                        sp.wait_ge(max_row_stored, rows)

                @block.tensor
                def _(pe):
                    for s in steps:
                        if s.kind in ("x_transpose", "qk_project", "v_project", "stack", "max_rows",
                                      "divide", "out_transpose", "out_project") and s.m:
                            pe.wait_ge(misc_taken, s.m)
                        if s.kind == "x_transpose":
                            if name == "prologue":
                                pe.wait_ge(x_loaded, 16)
                            elif s.n >= T:
                                pe.wait_ge(x_loaded, 16)
                            for k in range(KC):
                                ins = pe.transpose(misc_bank[:, k * P:(k + 1) * P], x_in[:, s.t, k * P:(k + 1) * P],
                                                   ident[:])
                            ins.then_inc(misc_filled, 1)
                        if s.kind == "qk_project":
                            for k in range(KC):
                                ins = pe.matmul(misc_bank[:, 0:2 * D], x_tr[:, k, :], w_qkv[:, k, 0:2 * D],
                                                start=(k == 0), stop=(k == KC - 1))
                            ins.then_inc(misc_filled, 1)
                        if s.kind == "v_project":
                            for k in range(KC):
                                ins = pe.matmul(misc_bank[:, 0:D], x_tr[:, k, :], w_qkv[:, k, 2 * D:3 * D],
                                                start=(k == 0), stop=(k == KC - 1))
                            ins.then_inc(misc_filled, 1)
                        if s.kind == "stack":
                            pe.wait_ge(lo_done, 2 * (s.n + 1))
                            pe.wait_ge(dup_done, 4 * (s.n + 1))
                            for w in range(2 * GRP):
                                ins = pe.transpose(misc_half[:, w * P:(w + 1) * P],
                                                   source[:, s.n % 2, w // GRP, w % GRP, :], ident_b[:])
                            ins.then_inc(misc_filled, 1)
                        if s.kind == "row_max":
                            if s.stack_need:
                                pe.wait_ge(misc_taken, s.stack_need)
                            if s.n >= 2:
                                pe.wait_ge(max_taken, s.n - 1)
                            q = stacks[0:STACK, s.slot, 0, s.j, s.t * P:(s.t + 1) * P]
                            for h in range(2):
                                k_rows = stacks[0:STACK, s.slot, 1, s.j, h * HALF:(h + 1) * HALF]
                                ins = pe.matmul(max_banks[s.n % 2][:, h, :], q, k_rows, start=True, stop=True)
                            ins.then_inc(max_scores, 1)
                        if s.kind == "max_rows":
                            pe.wait_ge(max_lo, s.n + 1)
                            pe.transpose(misc_half[0:GRP * MAXR * TH, 0:P], max_terms.rearrange("p a b c -> p (a b c)"),
                                         ident_b[:]).then_inc(misc_filled, 1)
                        if s.kind == "scores":
                            if s.rows_need:
                                pe.wait_ge(max_row_stored, s.rows_need)
                            if s.n >= 2:
                                pe.wait_ge(probs_ready, s.n - 1)
                            half, t = s.c // T, s.c % T
                            k_rows = stacks[0:STACK + MAXR, s.slot, 1, s.j, t * P:(t + 1) * P]
                            q = stacks[0:STACK + MAXR, s.slot, 0, s.j, half * HALF:(half + 1) * HALF]
                            pe.matmul(score_banks[s.n % 2], k_rows, q, start=True, stop=True).then_inc(scores_ready, 1)
                        if s.kind == "values":
                            t = s.c % T
                            pe.wait_ge(probs_ready, GRP * (s.n + 1))
                            if t == 0 and s.n >= T:
                                pe.wait_ge(values_copied, s.n // T)
                            for j in range(GRP):
                                ins = pe.matmul(value_bank[32 * j:32 * j + VW, :], v_ones[:, s.par, t, s.g * GRP + j, :],
                                                probs[:, GRP * (s.n % 2) + j, :], start=(t == 0), stop=(t == T - 1))
                            ins.then_inc(values_done, 1)
                        if s.kind == "divide":
                            if name == "body" and s.n >= 2:
                                pe.wait_ge(values_copied, s.n - 1)
                            for k in range(4):
                                q0 = (4 * s.half + k) * P
                                ins = pe.transpose(misc_bank[:, k * P:(k + 1) * P], values_tr[:, s.u, q0:q0 + P], ident[:])
                            ins.then_inc(misc_filled, 1)
                        if s.kind == "out_transpose":
                            for k in range(KC):
                                ins = pe.transpose(misc_bank[:, k * P:(k + 1) * P], attn[:, s.par, s.t, k * P:(k + 1) * P],
                                                   ident[:])
                            ins.then_inc(misc_filled, 1)
                        if s.kind == "out_project":
                            for k in range(KC):
                                ins = pe.matmul(misc_bank[:, 0:D], attn_tr[:, k, :], w_out[:, k, :],
                                                start=(k == 0), stop=(k == KC - 1))
                            ins.then_inc(misc_filled, 1)

                @block.scalar
                def _(act):
                    for s in steps:
                        if s.kind == "x_transpose":
                            act.wait_ge(misc_filled, s.m + 1)
                            act.copy(x_tr[:], misc_bank[:, 0:D].rearrange("p (k q) -> p k q", k=KC))\
                               .then_inc(misc_taken, 1)
                        if s.kind == "stack":
                            act.wait_ge(misc_filled, s.m + 1)
                            act.copy(stacks[:, s.slot, :, :, s.t * P:(s.t + 1) * P].rearrange("p w j q -> p (w j) q"),
                                     misc_half.rearrange("p (w q) -> p w q", w=2 * GRP)).then_inc(misc_taken, 1)
                        if s.kind == "max_rows":
                            act.wait_ge(misc_filled, s.m + 1)
                            if s.n:
                                act.wait_ge(max_row_stored, 16 * GRP * s.n)
                            act.copy(max_row[:], misc_half[0:GRP * MAXR * TH, 0:P]).then_inc(misc_taken, 1)
                        if s.kind == "scores":
                            act.wait_ge(scores_ready, s.n + 1)
                            if s.n >= 2 * GRP:
                                act.wait_ge(values_done, s.n // GRP - 1)
                            act.activation(probs[:, s.n % (2 * GRP)], score_banks[s.n % 2], ACT.Exp,
                                           scale=float(INV_SCALE)).then_inc(probs_ready, 1)
                        if s.kind == "values" and s.c % T == T - 1:
                            half = s.c // T
                            act.wait_ge(values_done, s.n + 1)
                            act.copy(values_tr[:, s.u % 2, half * HALF:(half + 1) * HALF], value_bank)\
                               .then_inc(values_copied, 1)
                        if s.kind == "out_transpose":
                            act.wait_ge(misc_filled, s.m + 1)
                            act.copy(attn_tr[:], misc_bank[:, 0:D].rearrange("p (k q) -> p k q", k=KC))\
                               .then_inc(misc_taken, 1)

                @block.vector
                def _(dve):
                    roped_at = {}
                    for s in steps:
                        if s.kind == "qk_project":
                            dve.wait_ge(misc_filled, s.m + 1)
                            if s.n:
                                dve.wait_ge(cos_done, s.n)
                                dve.wait_ge(sin_done, 2 * s.n)
                            dve.tensor_tensor(qk[:], misc_bank[:, 0:2 * D], bias[:, 0:2 * D], ALU.add)\
                               .then_inc(misc_taken, 1)
                            qk_m = s.m
                        if s.kind == "v_project":
                            dve.wait_ge(misc_filled, s.m + 1)
                            dve.tensor_tensor(v_ones[:, s.par, s.t, :, 0:HD1], heads(misc_bank[:, 0:D], H1),
                                              heads(bias[:, 2 * D:3 * D], H1), ALU.add).then_inc(misc_taken, 1)
                        if s.kind == "rope":
                            roped_at[s.par, s.t] = s.n + 1
                        if s.kind in ("split_1", "rest_1", "split_2", "split_3"):
                            rq = roped[:, s.par, s.t, :].rearrange("p (w h d) -> p w h d", w=2, h=H1)
                            rq = rq[:, :, s.g * GRP:(s.g + 1) * GRP, :]
                            src = terms(s.n % 2)
                        if s.kind == "split_1":
                            if (s.par, s.t) in roped_at:
                                dve.wait_ge(roped_done, roped_at[s.par, s.t])
                            if s.n >= 2:
                                dve.wait_ge(misc_filled, stack_m[s.n - 2] + 1)
                            dve.tensor_copy(src[:, :, :, 0, :], rq).then_inc(hi_done, 1)
                        if s.kind == "rest_1":
                            dve.wait_ge(hi_done, s.n + 1)
                            dve.tensor_tensor(rest[:], rq, src[:, :, :, 0, :], ALU.subtract).then_inc(rest_done, 1)
                        if s.kind == "split_2":
                            dve.wait_ge(rest_done, s.n + 1)
                            for w, at in enumerate((3, 1)):
                                dve.tensor_copy(src[:, w, :, at, :], rest[:, w]).then_inc(mid_done, 1)
                        if s.kind == "split_3":
                            dve.wait_ge(mid_done, 2 * (s.n + 1))
                            for w, (at, mid) in enumerate(((5, 3), (2, 1))):
                                dve.tensor_tensor(src[:, w, :, at, :], rest[:, w], src[:, w, :, mid, :], ALU.subtract)\
                                   .then_inc(lo_done, 1)
                        if s.kind == "row_max":
                            dve.wait_ge(max_scores, s.n + 1)
                            dve.tensor_reduce(row_max[:, s.j, s.t:s.t + 1], max_banks[s.n % 2], AX.XY, ALU.max, negate=True)\
                               .then_inc(max_taken, 1)
                        if s.kind == "max_hi":
                            if s.m:
                                dve.wait_ge(max_taken, s.m)
                            if s.n:
                                dve.wait_ge(misc_filled, max_m[s.n - 1] + 1)
                            tiles = slice(s.half * TH, (s.half + 1) * TH)
                            dve.tensor_copy(max_terms[:, :, 0, :], row_max[:, :, tiles]).then_inc(max_hi, 1)
                        if s.kind == "max_lo":
                            dve.wait_ge(max_hi, s.n + 1)
                            tiles = slice(s.half * TH, (s.half + 1) * TH)
                            dve.tensor_tensor(max_terms[:, :, 1, :], row_max[:, :, tiles], max_terms[:, :, 0, :], ALU.subtract)\
                               .then_inc(max_lo, 1)
                        if s.kind == "divide":
                            dve.wait_ge(misc_filled, s.m + 1)
                            dve.reciprocal(recip[:, s.n % 2], value_sums[:, :, :, HD1]).then_inc(recip_done, 1)
                        if s.kind == "divide_apply":
                            dve.wait_ge(recip_done, s.n + 1)
                            out = attn[:, s.par, 4 * s.half:4 * s.half + 4, s.g * GRP * HD1:(s.g + 1) * GRP * HD1]
                            dve.tensor_tensor(out.rearrange("p k (j d) -> p k j d", j=GRP), value_sums[:, :, :, 0:HD1],
                                              recip[:, s.n % 2].unsqueeze(3).to_broadcast([P, 4, GRP, HD1]), ALU.mult)\
                               .then_inc(misc_taken, 1)
                        if s.kind == "out_project":
                            dve.wait_ge(misc_filled, s.m + 1)
                            if i is not None and s.par == 0:
                                dve.wait_ge(residual_loaded, 16)
                            dve.tensor_tensor(res[:, s.n % 2], misc_bank[:, 0:D], x_res[:, s.par, s.t, :], ALU.add)\
                               .then_inc(misc_taken, 1)
                            res_m = s.m
                        if s.kind == "norm_stats":
                            dve.wait_ge(misc_taken, res_m + 1)
                            dve.bn_stats(stats[:, s.n % 2], res[:, s.n % 2]).then_inc(stats_done, 1)
                        if s.kind == "norm_mean":
                            dve.wait_ge(stats_done, s.n + 1)
                            if s.n >= 2:
                                dve.wait_ge(eps_done, s.n - 1)
                            dve.bn_aggr(mean_var[:, s.n % 2], stats[:, s.n % 2]).then_inc(mean_done, 1)
                        if s.kind == "norm_apply":
                            dve.wait_ge(rstd_done, s.n + 1)
                            if s.n >= 2:
                                dve.wait_ge(x1_stored[s.n % 2], 16 * (s.n // 2))
                            dve.tensor_scalar(x1_out[:, s.n % 2], res[:, s.n % 2], mean_var[:, s.n % 2, 0:1],
                                              rstd[:, s.n % 2], ALU.subtract, ALU.mult).then_inc(x1_ready, 1)

                @block.gpsimd
                def _(pool):
                    for s in steps:
                        if s.kind == "qk_project":
                            qk_m = s.m
                        if s.kind == "rope_cos":
                            pool.wait_ge(misc_taken, qk_m + 1)
                            if s.n:
                                pool.wait_ge(roped_done, s.n)
                            table = cos_t[:, s.t, :].unsqueeze(1).to_broadcast([P, 2 * H1, HD1])
                            pool.tensor_tensor(heads(by_cos[:], 2 * H1), heads(qk[:], 2 * H1), table,
                                               ALU.mult).then_inc(cos_done, 1)
                        if s.kind == "rope_sin":
                            pairs = qk[:].rearrange("p (h e two) -> p h e two", h=2 * H1, two=2)
                            outs = by_sin[:].rearrange("p (h e two) -> p h e two", h=2 * H1, two=2)
                            sins = sin_t[:, s.t, :].rearrange("p (e two) -> p e two", two=2)
                            for e in range(2):
                                table = sins[:, :, e].unsqueeze(1).to_broadcast([P, 2 * H1, HD1 // 2])
                                pool.tensor_tensor(outs[:, :, :, e], pairs[:, :, :, 1 - e], table, ALU.mult)\
                                    .then_inc(sin_done, 1)
                        if s.kind == "rope":
                            pool.wait_ge(cos_done, s.n + 1)
                            pool.wait_ge(sin_done, 2 * (s.n + 1))
                            pool.tensor_tensor(roped[:, s.par, s.t, :], by_cos[:], by_sin[:], ALU.add)\
                                .then_inc(roped_done, 1)
                        if s.kind == "split_1":
                            pool.wait_ge(hi_done, s.n + 1)
                            src = terms(s.n % 2)
                            for w, at in enumerate((slice(1, 3), slice(3, 6, 2))):
                                first = src[:, w, :, 0:1, :].to_broadcast([P, GRP, 2, HD1])
                                pool.tensor_copy(src[:, w, :, at, :], first).then_inc(dup_done, 1)
                        if s.kind == "split_2":
                            src = terms(s.n % 2)
                            pool.wait_ge(mid_done, 2 * (s.n + 1))
                            for w, mid in enumerate((3, 1)):
                                pool.tensor_copy(src[:, w, :, 4, :], src[:, w, :, mid, :]).then_inc(dup_done, 1)
                        if s.kind == "norm_mean":
                            pool.wait_ge(mean_done, s.n + 1)
                            if s.n >= 2:
                                pool.wait_ge(x1_ready, s.n - 1)
                            pool.tensor_scalar(var_eps[:, s.n % 2], mean_var[:, s.n % 2, 1:2], LN_EPS, None, ALU.add)\
                                .then_inc(eps_done, 1)
                            pool.wait_ge(eps_done, s.n + 1)
                            pool.tensor_tensor(rstd[:, s.n % 2], var_eps[:, s.n % 2], minus_half[:], ALU.pow)\
                                .then_inc(rstd_done, 1)

            nc.all_engine_barrier(sems_to_clear=range(min(sem_nums), max(sem_nums) + 1))

        sem_nums = [s.num for s in sems]

        with nc.Block() as block:
            @block.sync
            def _(sp):
                sp.dma_start(w_qkv[:], wqkv_t.rearrange("(k p) n -> p k n", p=P)).then_inc(constants_loaded, 16)
                sp.dma_start(w_out[:], wo_t.rearrange("(k p) n -> p k n", p=P)).then_inc(constants_loaded, 16)
                sp.dma_start(bias[:], bqkv.partition_broadcast(P)).then_inc(constants_loaded, 16)
                sp.dma_start(cos_t[:], rope_cos.rearrange("(t p) e -> p t e", p=P)).then_inc(constants_loaded, 16)
                sp.dma_start(sin_t[:], rope_sin.rearrange("(t p) e -> p t e", p=P)).then_inc(constants_loaded, 16)
                sp.dma_start(ident[:], ident_in).then_inc(constants_loaded, 16)
                sp.wait_ge(constants_loaded, 96)

            @block.vector
            def _(dve):
                dve.memset(value_bank, 0.0)
                dve.memset(source[:, :, :, :, STACK:P], 0.0).then_inc(preset, 1)
                dve.wait_ge(preset, 1)
                dve.memset(source[:, :, 1, :, STACK:STACK + MAXR], 1.0)
                dve.wait_ge(constants_loaded, 96)
                dve.tensor_copy(ident_b[:], ident[:])
                dve.memset(minus_half[:], -0.5)

            @block.gpsimd
            def _(pool):
                pool.memset(v_ones[:, :, :, :, HD1:VW], 1.0)
                pool.memset(x_res[:, 1], 0.0)
                pool.memset(values_tr[:, 1], 1.0)
                pool.memset(attn[:, 1], 0.0)
        section("prologue")
        with nc.Fori(0, B // 2) as i:
            section("body", i)
        section("epilogue")


H2 = 8
HD2 = 64
INNER = H2 * HD2
WINDOW = 128
HID = int(D * 4 * 2 / 3)
HCH = 6
HCW = -(-HID // HCH)
OC = INNER // P
MGRP = 4
BODY = 2 * T
STAGES = 4
QK_SCALE = 8.0
MASKED = 1e37



def plan_layer(section, last):
    steps = []
    low, high = (0 if section == "first" else -BODY), (0 if section == "last" else 2 * BODY)

    def add(kind, n, part=0):
        if low <= n < high:
            steps.append(Step(kind, n=n, part=part))

    if section == "first":
        for n in range(5):
            add("load", n)
        add("h_transpose", 0)
    for s in range(BODY if section != "last" else 2 * MGRP):
        group, phase = (s - 7) // MGRP * MGRP, (s - 7) % MGRP
        add("load", s + 5)
        add("turn_q", s - 1)
        add("ln_apply", s - 4)
        add("bias", s - 5)
        add("wo", s - 3)
        add("y_shift", s - 3)
        add("turn_k", s - 1)
        add("exp", s - 2, 3)
        add("h_transpose", s + 1)
        add("project_q", s)
        add("scale", s - 2, 3)
        add("p_transpose", s - 2, 0)
        add("project_k", s)
        add("squares", s)
        add("window_scores", s - 1, 0)
        add("ln_transpose", s - 4)
        add("attend", s - 2, 0)
        add("p_transpose", s - 2, 1)
        add("exp", s - 1, 0)
        if phase == 3:
            add("mlp_out", group)
        add("window_scores", s - 1, 1)
        add("rope_sin", s)
        add("y_stats", s - 3)
        add("attend", s - 2, 1)
        add("p_transpose", s - 2, 2)
        add("exp", s - 1, 1)
        add("scale", s - 1, 0)
        if phase == 3:
            add("finish_mean", group)
            add("mlp_out", group + 1)
        add("window_scores", s - 1, 2)
        add("attend", s - 2, 2)
        add("p_transpose", s - 2, 3)
        add("exp", s - 1, 2)
        if phase == 3:
            add("finish_mean", group + 1)
            add("mlp_out", group + 2)
        add("window_scores", s - 1, 3)
        add("rope_cos", s)
        add("project_v", s)
        add("scale", s - 1, 1)
        if phase == 3:
            add("attend", s - 2, 3)
        add("scale", s - 1, 2)
        if last and phase == 2:
            for k in range(MGRP):
                add("load_x1", group + k)
        if phase < 3:
            add("mlp_in", group, 2 * phase)
            add("attend", s - 2, 3)
            add("o_split", s - 2)
            add("mlp_in", group, 2 * phase + 1)
        else:
            add("o_split", s - 2)
            add("finish_mean", group + 2)
            add("mlp_out", group + 3)
            add("finish_mean", group + 3)
        if phase == (0 if last else 3):
            for k in range(MGRP):
                add("finish", group + k - (MGRP if last else 0))
    return steps


SMALL_USES = ("h_transpose", "ln_transpose")
OUT_USES = ("project_v", "wo", "mlp_out")
TURN_USES = ("turn_q", "turn_k", "p_transpose")


def layer_pass(nc, layer, last, x_src, x1_src, dst, wqkv, q_scale, k_scale, wo, ln_g, ln_b, w1, b1, w2, b2,
               tables, mask_in, ident_in):
    with ExitStack() as ctx:
        def sb(name, shape, dt=F32):
            return ctx.enter_context(nc.sbuf_tensor(f"l{layer}_{name}", shape, dt))

        sems = []

        def sem(name):
            s = ctx.enter_context(nc.semaphore(f"l{layer}_{name}"))
            sems.append(s)
            return s

        psum = ctx.enter_context(nc.psum_tensor(f"l{layer}_psum", [P, 8, HALF], F32))
        qk_banks = psum[:, 0:2, :]
        out_bank = psum[:, 2, :]
        small_bank = psum[:, 3, :]
        pair_banks = [psum[:, 4, :], psum[:, 5, :]]
        turn_bank = psum[:, 6, :]
        attend_bank = psum[:, 7, :]

        wqkv_t = [sb(f"wqkv_{k}", [P, KC, 3 * INNER], F32R) for k in range(2)]
        wo_t = [sb(f"wo_{k}", [P, OC, D], F32R) for k in range(2)]
        w1_t = [sb(f"w1_{k}", [P, KC, 2 * HID], F32R) for k in range(2)]
        w2_t = [sb(f"w2_{k}", [HCW, HCH, D], F32R) for k in range(2)]
        mask = sb("mask", [P, 2, 2 * P])
        ident = sb("ident", [P, P])
        rope_c = sb("rope_c", [P, T, 2, HD2])
        rope_s = sb("rope_s", [P, T, 2, HD2])
        gain = sb("gain", [P, KC])
        shift = sb("shift", [P, KC])
        b1_a = sb("b1_a", [HCW, HCH])
        b1_g = sb("b1_g", [HCW, HCH])
        b2_all = sb("b2_all", [P, D])
        scales = sb("scales", [P, 2, HD2])
        exponent = sb("exponent", [P, 2 * H2])
        zero_col = sb("zero_col", [P, 1])
        zero_row = sb("zero_row", [1, P])
        table_warm = sb("table_warm", [P, 1])
        x = sb("x", [P, T, D])
        y = sb("y", [P, T, D])
        h_t = [sb(f"h_t_{k}", [P, 2, KC, P + 1], F32R) for k in range(2)]
        work_a = sb("work_a", [P, 2, H2, HD2])
        work_b = sb("work_b", [P, 2, H2, HD2])
        rot = sb("rot", [P, 2 * INNER])
        squares_sum = sb("squares_sum", [P, 2, 2 * H2])
        clipped = sb("clipped", [P, 2, 2 * H2])
        inv_norm = sb("inv_norm", [P, 2, 2 * H2])
        q_t = sb("q_t", [P, OC, P])
        k_t = sb("k_t", [P, 4, OC, P])
        v = sb("v", [P, 4, INNER])
        probs = sb("probs", [P, H2, 2 * P])
        neg_max = sb("neg_max", [P, 2, H2])
        sums = sb("sums", [P, 2, H2])
        inv_sums = sb("inv_sums", [P, 2, H2])
        probs_t = sb("probs_t", [P, 2, 4, P])
        o_t = [sb(f"o_t_{k}", [P, OC, P], F32R) for k in range(2)]
        normed = sb("normed", [P, 2, D])
        stats = sb("stats", [P, 2, 2, 6])
        mean_var = sb("mean_var", [P, 2, 2])
        var_eps = sb("var_eps", [P, 2, 1])
        rstd = sb("rstd", [P, 2, 1])
        ln_full = sb("ln_full", [P, KC, P])
        ln_t = [sb(f"ln_t_{k}", [P, 2, KC, MGRP * P], F32R) for k in range(2)]
        gate = sb("gate", [HCW, MGRP * P])
        hid_full = sb("hid_full", [HCW, MGRP * P])
        hid = [sb(f"hid_{k}", [HCW, HCH, MGRP * P], F32R) for k in range(2)]
        x_out = sb("x_out", [P, MGRP, D])
        x1_in = sb("x1_in", [P, MGRP, D]) if last else None
        f_stats = sb("f_stats_t", [P, MGRP, 6])
        f_mean_var = sb("f_mean_var", [P, MGRP, 2])
        f_var_eps = sb("f_var_eps", [P, MGRP, 1])
        f_rstd = sb("f_rstd", [P, MGRP, 1])

        constants_loaded = sem("constants_loaded")
        stage_loaded = [sem(f"stage_loaded_{k}") for k in range(STAGES)]
        stage_hi = sem("stage_hi")
        stage_lo = sem("stage_lo")
        preset = sem("preset")
        x_loaded = [sem(f"x_loaded_{k}") for k in range(T)]
        small_filled, small_taken = sem("small_filled"), sem("small_taken")
        out_filled, out_taken = sem("out_filled"), sem("out_taken")
        turn_filled, turn_taken = sem("turn_filled"), sem("turn_taken")
        h_hi, h_lo = sem("h_hi"), sem("h_lo")
        q_ready, k_ready = sem("q_ready"), sem("k_ready")
        squared = sem("squared")
        squares_summed = sem("squares_summed")
        norms_clipped, norms_ready = sem("norms_clipped"), sem("norms_ready")
        by_cos_done, by_sin_done = sem("by_cos_done"), sem("by_sin_done")
        rope_added, rotated = sem("rope_added"), sem("rotated")
        pair_filled = sem("pair_filled")
        max_done = sem("max_done")
        exp_done = sem("exp_done")
        sums_inverted = sem("sums_inverted")
        probs_scaled = sem("probs_scaled")
        attend_done = sem("attend_done")
        o_hi, o_lo = sem("o_hi"), sem("o_lo")
        y_shifted = [sem(f"y_shifted_{k}") for k in range(2)]
        ln_scaled = sem("ln_scaled")
        y_stats, y_mean, y_eps, y_rstd, y_normed = (sem(k) for k in ("y_stats", "y_mean", "y_eps", "y_rstd", "y_normed"))
        ln_hi, ln_lo = sem("ln_hi"), sem("ln_lo")
        y_biased = sem("y_biased")
        gated = sem("gated")
        warmed = sem("warmed")
        hid_product, hid_hi, hid_lo = sem("hid_product"), sem("hid_hi"), sem("hid_lo")
        x1_loaded = [sem(f"x1_loaded_{k}") for k in range(MGRP)]
        f_summed, f_stats_done, f_mean, f_eps, f_rstd_done = (
            sem(k) for k in ("f_summed", "f_stats", "f_mean", "f_eps", "f_rstd_done"))
        x_out_ready = sem("x_out_ready")
        stored = [sem(f"stored_{k}") for k in range(MGRP)]

        def tile_of(dram, i, n):
            flat = dram.rearrange("b (t p) d -> (b t) p d", p=P)
            tile = BODY * i + n
            return flat[tile % (B * T) if n >= BODY else tile]

        def three(eng, out, left, right, first, final):
            eng.matmul(out, left[0], right[0], start=first, stop=False)
            eng.matmul(out, left[0], right[1], start=False, stop=False)
            return eng.matmul(out, left[1], right[0], start=False, stop=final)

        def section(name, i):
            steps = plan_layer(name, last)
            counts, made, used, pair_uses = {}, {}, {}, []
            loaded, shifts, x1_loads, stores = {}, {}, {}, {}
            for s in steps:
                counts[s.kind] = counts.get(s.kind, 0) + 1
                s.count = made[s.kind, s.n, s.part] = counts[s.kind]
                for bank, kinds in (("small", SMALL_USES), ("out", OUT_USES), ("turn", TURN_USES)):
                    if s.kind in kinds:
                        s.use = counts.get(bank, 0)
                        counts[bank] = used[s.kind, s.n, s.part] = s.use + 1
                if s.kind == "window_scores":
                    s.pair = len(pair_uses)
                    pair_uses.append((max_done, 2 * s.count))
                if s.kind == "mlp_in":
                    s.pair = len(pair_uses)
                    pair_uses += [(gated, s.count), (hid_product, s.count)]
                for kind, done, slots, per in (("load", loaded, T, 16), ("y_shift", shifts, 2, 32),
                                               ("load_x1", x1_loads, MGRP, 16), ("finish", stores, MGRP, 16)):
                    if s.kind == kind:
                        done[s.n] = per * (1 + sum(m % slots == s.n % slots for m in done))

            def after(eng, semaphore, kind, n, part=0, per=1):
                if (kind, n, part) in made:
                    eng.wait_ge(semaphore, per * made[kind, n, part])

            def after_use(eng, semaphore, kind, n, part=0):
                if (kind, n, part) in used:
                    eng.wait_ge(semaphore, used[kind, n, part])

            def windows(t):
                return (0, 1) if t else (1,)

            def place(part, h):
                return slice(part % 2 * HD2, (part % 2 + 1) * HD2), part // 2 * 2 + h

            with nc.Block() as block:
                @block.sync
                def _(sp):
                    for s in steps:
                        n = s.n
                        if s.kind == "load":
                            after_use(sp, out_taken, "wo", n - T)
                            sp.dma_start(x[:, n % T, :], tile_of(x_src, i, n)).then_inc(x_loaded[n % T], 16)
                        if s.kind == "y_shift":
                            after_use(sp, out_taken, "wo", n)
                            after_use(sp, small_filled, "ln_transpose", n - 2)
                            to = normed[:, n % 2, P:D]
                            first = y[P - 1:P, (n - 1) % T, P:D] if n % T else zero_row[:]
                            sp.dma_start(to[0:1], first).then_inc(y_shifted[n % 2], 16)
                            sp.dma_start(to[1:P], y[0:P - 1, n % T, P:D]).then_inc(y_shifted[n % 2], 16)
                        if s.kind == "load_x1":
                            after(sp, f_summed, "mlp_out", n - MGRP)
                            sp.dma_start(x1_in[:, n % MGRP], tile_of(x1_src, i, n)).then_inc(x1_loaded[n % MGRP], 16)
                        if s.kind == "finish":
                            if last:
                                sp.wait_ge(x_out_ready, s.count)
                            else:
                                after_use(sp, out_taken, "mlp_out", n)
                            sp.dma_start(tile_of(dst, i, n), x_out[:, n % MGRP]).then_inc(stored[n % MGRP], 16)
                    for kind, done, per in (("finish", stored, 16), ("load_x1", x1_loaded, 16), ("load", x_loaded, 16),
                                            ("y_shift", y_shifted, 32)):
                        for k, semaphore in enumerate(done):
                            uses = sum(s.kind == kind and s.n % len(done) == k for s in steps)
                            if uses:
                                sp.wait_ge(semaphore, per * uses)

                @block.tensor
                def _(pe):
                    for s in steps:
                        n, t = s.n, s.n % T
                        if s.kind in SMALL_USES and s.use:
                            pe.wait_ge(small_taken, s.use)
                        if s.kind in OUT_USES and s.use:
                            pe.wait_ge(out_taken, s.use)
                        if s.kind in TURN_USES and s.use:
                            pe.wait_ge(turn_taken, s.use)
                        if s.kind == "h_transpose":
                            if n in loaded:
                                pe.wait_ge(x_loaded[n % T], loaded[n])
                            for k in range(KC):
                                ins = pe.transpose(small_bank[:, k * P:(k + 1) * P], x[:, n % T, k * P:(k + 1) * P], ident[:])
                            ins.then_inc(small_filled, 1)
                        if s.kind in ("project_q", "project_k", "project_v"):
                            part = ("project_q", "project_k", "project_v").index(s.kind)
                            after(pe, h_hi, "h_transpose", n, per=2)
                            after(pe, h_lo, "h_transpose", n)
                            if part < 2:
                                after(pe, by_cos_done, "rope_cos", n - 1)
                                after(pe, by_sin_done, "rope_sin", n - 1, per=2)
                            out = out_bank if part == 2 else qk_banks[:, part, :]
                            for k in range(KC):
                                left = [h_t[e][:, n % 2, k, 1 - k:1 - k + P] for e in range(2)]
                                right = [wqkv_t[e][:, k, part * INNER:(part + 1) * INNER] for e in range(2)]
                                ins = three(pe, out, left, right, k == 0, k == KC - 1)
                            ins.then_inc((q_ready, k_ready, out_filled)[part], 1)
                        if s.kind in ("turn_q", "turn_k"):
                            if ("rope_cos", n, 0) in made:
                                pe.wait_ge(rotated, 2 * made["rope_cos", n, 0] - (s.kind == "turn_q"))
                            for k in range(OC):
                                at = (s.kind == "turn_k") * INNER + k * P
                                ins = pe.transpose(turn_bank[:, k * P:(k + 1) * P], rot[:, at:at + P], ident[:])
                            ins.then_inc(turn_filled, 1)
                        if s.kind == "window_scores":
                            after_use(pe, turn_taken, "turn_k", n)
                            if s.pair >= 2:
                                pe.wait_ge(*pair_uses[s.pair - 2])
                            bank = pair_banks[s.pair % 2]
                            for h in range(2):
                                rows, chunk = place(s.part, h)
                                for w in windows(t):
                                    at = (2 * h + w) * P
                                    ins = pe.matmul(bank[:, at:at + P], q_t[rows, chunk, :],
                                                    k_t[rows, (n - 1 + w) % 4, chunk, :], start=True, stop=True)
                            ins.then_inc(pair_filled, 1)
                        if s.kind == "p_transpose":
                            after(pe, probs_scaled, "scale", n, s.part, per=2)
                            for h in range(2):
                                for w in windows(t):
                                    at = (2 * h + w) * P
                                    ins = pe.transpose(turn_bank[:, at:at + P],
                                                       probs[:, 2 * s.part + h, w * P:(w + 1) * P], ident[:])
                            ins.then_inc(turn_filled, 1)
                        if s.kind == "attend":
                            after_use(pe, turn_taken, "p_transpose", n, s.part)
                            if s.part == 0:
                                after(pe, o_lo, "o_split", n - 1)
                            for h in range(2):
                                rows, chunk = place(s.part, h)
                                for w in windows(t):
                                    ins = pe.matmul(attend_bank[rows, chunk * P:(chunk + 1) * P],
                                                    v[:, (n - 1 + w) % 4, chunk * P + rows.start:chunk * P + rows.stop],
                                                    probs_t[:, s.part % 2, 2 * h + w, :],
                                                    start=(w == windows(t)[0]), stop=(w == 1))
                            ins.then_inc(attend_done, 1)
                        if s.kind == "wo":
                            after(pe, o_lo, "o_split", n)
                            for k in range(OC):
                                ins = three(pe, out_bank[:, 0:D], [o_t[e][:, k, :] for e in range(2)],
                                            [wo_t[e][:, k, :] for e in range(2)], k == 0, k == OC - 1)
                            ins.then_inc(out_filled, 1)
                        if s.kind == "ln_transpose":
                            after(pe, y_normed, "ln_apply", n, per=2)
                            for k in range(KC):
                                ins = pe.transpose(small_bank[:, k * P:(k + 1) * P], normed[:, n % 2, k * P:(k + 1) * P],
                                                   ident[:])
                            ins.then_inc(small_filled, 1)
                        if s.kind == "mlp_in":
                            after(pe, ln_lo, "ln_transpose", n + MGRP - 1)
                            width = min(HCW, HID - s.part * HCW)
                            for half in range(2):
                                if s.pair + half >= 2:
                                    pe.wait_ge(*pair_uses[s.pair + half - 2])
                                cols = (1 - half) * HID + s.part * HCW
                                out = pair_banks[(s.pair + half) % 2][0:width, :]
                                for k in range(KC):
                                    ins = three(pe, out, [w1_t[e][:, k, cols:cols + width] for e in range(2)],
                                                [ln_t[e][:, n // MGRP % 2, k, :] for e in range(2)], k == 0, k == KC - 1)
                                ins.then_inc(pair_filled, 1)
                        if s.kind == "mlp_out":
                            after(pe, hid_lo, "mlp_in", n // MGRP * MGRP, HCH - 1)
                            for k in range(HCH):
                                width = min(HCW, HID - k * HCW)
                                cols = slice(n % MGRP * P, (n % MGRP + 1) * P)
                                ins = three(pe, out_bank[:, 0:D], [hid[e][0:width, k, cols] for e in range(2)],
                                            [w2_t[e][0:width, k, :] for e in range(2)], k == 0, k == HCH - 1)
                            ins.then_inc(out_filled, 1)

                @block.scalar
                def _(act):
                    for s in steps:
                        n, t = s.n, s.n % T
                        if s.kind == "h_transpose":
                            act.wait_ge(small_filled, s.use + 1)
                            act.copy(h_t[0][:, n % 2, :, 1:P + 1], small_bank[:, 0:D].rearrange("p (k q) -> p k q", k=KC))\
                               .then_inc(h_hi, 1)
                            before = h_t[0][:, (n - 1) % 2, 1, P:P + 1].bitcast(F32) if t else zero_col[:]
                            after(act, h_hi, "h_transpose", n - 1, per=2)
                            act.copy(h_t[0][:, n % 2, 1, 0:1], before).then_inc(h_hi, 1)
                        if s.kind == "project_v":
                            act.wait_ge(out_filled, s.use + 1)
                            act.copy(v[:, n % 4, :], out_bank).then_inc(out_taken, 1)
                        if s.kind == "squares":
                            act.wait_ge(q_ready, s.count)
                            act.wait_ge(k_ready, s.count)
                            after(act, rotated, "rope_cos", n - 1, per=2)
                            act.square(work_a.rearrange("p w h d -> p (w h d)"),
                                       qk_banks.rearrange("p w c -> p (w c)")).then_inc(squared, 1)
                        if s.kind in ("turn_q", "turn_k"):
                            act.wait_ge(turn_filled, s.use + 1)
                            out = q_t[:] if s.kind == "turn_q" else k_t[:, n % 4]
                            act.copy(out, turn_bank.rearrange("p (k q) -> p k q", k=OC)).then_inc(turn_taken, 1)
                        if s.kind == "p_transpose":
                            act.wait_ge(turn_filled, s.use + 1)
                            after(act, attend_done, "attend", *((n, s.part - 2) if s.part >= 2 else (n - 1, s.part + 2)))
                            src = turn_bank.rearrange("p (h w q) -> p h w q", h=2, w=2)
                            out = probs_t[:, s.part % 2].rearrange("p (h w) q -> p h w q", h=2)
                            first = windows(t)[0]
                            act.copy(out[:, :, first:2, :], src[:, :, first:2, :]).then_inc(turn_taken, 1)
                        if s.kind == "exp":
                            after(act, max_done, "window_scores", n, s.part, per=2)
                            keys = slice(windows(t)[0] * P, 2 * P)
                            for h in range(2):
                                head = 2 * s.part + h
                                act.activation(probs[:, head, keys], probs[:, head, keys], ACT.Exp,
                                               scale=-1.0, bias=neg_max[:, n % 2, head:head + 1],
                                               accum_out=sums[:, n % 2, head:head + 1]).then_inc(exp_done, 1)
                        if s.kind == "o_split":
                            after(act, attend_done, "attend", n, 3)
                            act.copy(o_t[0][:], attend_bank.rearrange("p (k q) -> p k q", k=OC)).then_inc(o_hi, 1)
                        if s.kind == "ln_transpose":
                            act.wait_ge(small_filled, s.use + 1)
                            if s.count > 1:
                                act.wait_ge(ln_lo, s.count - 1)
                            for k, done in enumerate((ln_scaled, small_taken)):
                                act.activation(ln_full[:, k, :], small_bank[:, k * P:(k + 1) * P], ACT.Identity,
                                               scale=gain[:, k:k + 1], bias=shift[:, k:k + 1]).then_inc(done, 1)
                        if s.kind == "mlp_in":
                            if s.part % 2 == 0:
                                if s.count > 1:
                                    act.wait_ge(warmed, s.count - 1)
                                act.activation(table_warm[:], zero_col[:], ACT.Gelu).then_inc(warmed, 1)
                            act.wait_ge(pair_filled, s.pair + 1)
                            if s.count > 1:
                                act.wait_ge(hid_product, s.count - 1)
                            width = min(HCW, HID - s.part * HCW)
                            act.activation(gate[0:width, :], pair_banks[s.pair % 2][0:width, :], ACT.Gelu,
                                           bias=b1_g[0:width, s.part:s.part + 1]).then_inc(gated, 1)
                            if s.part % 2:
                                act.wait_ge(warmed, s.count - 1)
                                act.activation(table_warm[:], zero_col[:], ACT.Exp).then_inc(warmed, 1)

                @block.vector
                def _(dve):
                    for s in steps:
                        n, t = s.n, s.n % T
                        if s.kind == "h_transpose":
                            dve.wait_ge(h_hi, 2 * s.count - 1)
                            dve.tensor_tensor(h_t[1][:, n % 2, :, 1:P + 1], small_bank[:, 0:D].rearrange("p (k q) -> p k q", k=KC),
                                              h_t[0][:, n % 2, :, 1:P + 1].bitcast(F32), ALU.subtract).then_inc(small_taken, 1)
                            before = h_t[1][:, (n - 1) % 2, 1, P:P + 1].bitcast(F32) if t else zero_col[:]
                            after_use(dve, small_taken, "h_transpose", n - 1)
                            dve.tensor_copy(h_t[1][:, n % 2, 1, 0:1], before).then_inc(h_lo, 1)
                        if s.kind == "squares":
                            dve.wait_ge(squared, s.count)
                            dve.tensor_reduce(squares_sum[:, n % 2, :], work_a.rearrange("p w h d -> p (w h) d"), AX.X, ALU.add)\
                               .then_inc(squares_summed, 1)
                        if s.kind == "rope_sin":
                            if s.count > 1:
                                dve.wait_ge(rope_added, 2 * s.count - 2)
                            qk = qk_banks.rearrange("p w (h d) -> p w h d", h=H2)
                            table = rope_s[:, t].unsqueeze(2).to_broadcast([P, 2, H2, HD2])
                            for e in range(2):
                                to, of = slice(32 * e, 32 * e + 32), slice(32 - 32 * e, 64 - 32 * e)
                                dve.tensor_tensor(work_b[:, :, :, to], qk[:, :, :, of], table[:, :, :, to], ALU.mult)\
                                   .then_inc(by_sin_done, 1)
                        if s.kind == "rope_cos":
                            table = rope_c[:, t].unsqueeze(2).to_broadcast([P, 2, H2, HD2])
                            dve.wait_ge(squares_summed, s.count)
                            dve.tensor_tensor(work_a[:], qk_banks.rearrange("p w (h d) -> p w h d", h=H2), table, ALU.mult)\
                               .then_inc(by_cos_done, 1)
                        if s.kind == "window_scores":
                            dve.wait_ge(pair_filled, s.pair + 1)
                            keys, heads = slice(windows(t)[0] * P, 2 * P), slice(2 * s.part, 2 * s.part + 2)
                            scores = pair_banks[s.pair % 2].rearrange("p (h k) -> p h k", h=2)
                            for h in range(2):
                                head = 2 * s.part + h
                                dve.tensor_tensor_reduce(probs[:, head, keys], scores[:, h, keys], mask[:, h, keys], 1.0, MASKED,
                                                         ALU.add, ALU.min, neg_max[:, n % 2, head:head + 1])\
                                   .then_inc(max_done, 1)
                        if s.kind == "scale":
                            after(dve, exp_done, "exp", n, s.part, per=2)
                            heads = slice(2 * s.part, 2 * s.part + 2)
                            dve.reciprocal(inv_sums[:, n % 2, heads], sums[:, n % 2, heads]).then_inc(sums_inverted, 1)
                            dve.wait_ge(sums_inverted, s.count)
                            keys = slice(windows(t)[0] * P, 2 * P)
                            for head in range(2 * s.part, 2 * s.part + 2):
                                dve.tensor_scalar(probs[:, head, keys], probs[:, head, keys], inv_sums[:, n % 2, head:head + 1],
                                                  None, ALU.mult).then_inc(probs_scaled, 1)
                        if s.kind == "o_split":
                            dve.wait_ge(o_hi, s.count)
                            dve.tensor_tensor(o_t[1][:], attend_bank.rearrange("p (k q) -> p k q", k=OC),
                                              o_t[0][:].bitcast(F32), ALU.subtract).then_inc(o_lo, 1)
                        if s.kind == "wo":
                            dve.wait_ge(out_filled, s.use + 1)
                            if n in loaded:
                                dve.wait_ge(x_loaded[n % T], loaded[n])
                            dve.tensor_tensor(y[:, n % T, :], out_bank[:, 0:D], x[:, n % T, :], ALU.add).then_inc(out_taken, 1)
                        if s.kind == "y_stats":
                            after_use(dve, out_taken, "wo", n)
                            dve.bn_stats(stats[:, n % 2, 0, :], y[:, n % T, 0:P]).then_inc(y_stats, 1)
                            if n in shifts:
                                dve.wait_ge(y_shifted[n % 2], shifts[n])
                            dve.bn_stats(stats[:, n % 2, 1, :], normed[:, n % 2, P:D]).then_inc(y_stats, 1)
                            dve.wait_ge(y_stats, 2 * s.count)
                            if s.count > 2:
                                dve.wait_ge(y_eps, s.count - 2)
                            dve.bn_aggr(mean_var[:, n % 2], stats[:, n % 2].rearrange("p a b -> p (a b)")).then_inc(y_mean, 1)
                        if s.kind == "ln_apply":
                            after(dve, y_rstd, "y_stats", n)
                            for k, src in enumerate((y[:, n % T, 0:P], normed[:, n % 2, P:D])):
                                dve.tensor_scalar(normed[:, n % 2, k * P:(k + 1) * P], src, mean_var[:, n % 2, 0:1],
                                                  rstd[:, n % 2], ALU.subtract, ALU.mult).then_inc(y_normed, 1)
                        if s.kind == "ln_transpose":
                            dve.wait_ge(ln_scaled, s.count)
                            dve.wait_ge(small_taken, s.use + 1)
                            at = slice(n % MGRP * P, (n % MGRP + 1) * P)
                            hi, lo = (ln_t[e][:, n // MGRP % 2, :, at] for e in range(2))
                            dve.tensor_copy(hi, ln_full[:]).then_inc(ln_hi, 1)
                            dve.wait_ge(ln_hi, s.count)
                            dve.tensor_tensor(lo, ln_full[:], hi.bitcast(F32), ALU.subtract).then_inc(ln_lo, 1)
                        if s.kind == "mlp_in":
                            width = min(HCW, HID - s.part * HCW)
                            dve.wait_ge(gated, s.count)
                            if s.count > 1:
                                dve.wait_ge(hid_lo, s.count - 1)
                            dve.wait_ge(pair_filled, s.pair + 2)
                            dve.scalar_tensor_tensor(hid_full[0:width, :], pair_banks[(s.pair + 1) % 2][0:width, :],
                                                     b1_a[0:width, s.part:s.part + 1], gate[0:width, :], ALU.add, ALU.mult)\
                               .then_inc(hid_product, 1)
                            hi, lo = (hid[e][0:width, s.part, :] for e in range(2))
                            dve.wait_ge(hid_product, s.count)
                            dve.tensor_copy(hi, hid_full[0:width, :]).then_inc(hid_hi, 1)
                            dve.wait_ge(hid_hi, s.count)
                            dve.tensor_tensor(lo, hid_full[0:width, :], hi.bitcast(F32), ALU.subtract).then_inc(hid_lo, 1)
                        if s.kind == "mlp_out":
                            dve.wait_ge(out_filled, s.use + 1)
                            after(dve, y_biased, "bias", n)
                            if n - MGRP in stores:
                                dve.wait_ge(stored[n % MGRP], stores[n - MGRP])
                            dve.tensor_tensor(x_out[:, n % MGRP], out_bank[:, 0:D], y[:, n % T, :], ALU.add)\
                               .then_inc(out_taken, 1)
                            if last:
                                dve.wait_ge(out_taken, s.use + 1)
                                if n in x1_loads:
                                    dve.wait_ge(x1_loaded[n % MGRP], x1_loads[n])
                                dve.tensor_tensor(x_out[:, n % MGRP], x_out[:, n % MGRP], x1_in[:, n % MGRP], ALU.add)\
                                   .then_inc(f_summed, 1)
                        if s.kind == "finish_mean" and last:
                            after(dve, f_summed, "mlp_out", n)
                            dve.bn_stats(f_stats[:, n % MGRP], x_out[:, n % MGRP]).then_inc(f_stats_done, 1)
                            dve.wait_ge(f_stats_done, s.count)
                            if s.count > MGRP:
                                dve.wait_ge(f_eps, s.count - MGRP)
                            dve.bn_aggr(f_mean_var[:, n % MGRP], f_stats[:, n % MGRP]).then_inc(f_mean, 1)
                        if s.kind == "finish" and last:
                            after(dve, f_rstd_done, "finish_mean", n)
                            dve.tensor_scalar(x_out[:, n % MGRP], x_out[:, n % MGRP], f_mean_var[:, n % MGRP, 0:1],
                                              f_rstd[:, n % MGRP], ALU.subtract, ALU.mult).then_inc(x_out_ready, 1)

                @block.gpsimd
                def _(pool):
                    def inverse_root(of, plus_eps, out, eps_done, root_done, count):
                        pool.tensor_scalar(plus_eps, of, LN_EPS, None, ALU.add).then_inc(eps_done, 1)
                        pool.wait_ge(eps_done, count)
                        pool.tensor_tensor(out, plus_eps, exponent[:, 0:1], ALU.pow).then_inc(root_done, 1)

                    for s in steps:
                        n = s.n
                        if s.kind == "squares":
                            pool.wait_ge(squares_summed, s.count)
                            pool.tensor_scalar(clipped[:, n % 2], squares_sum[:, n % 2], 1e-24, None, ALU.max)\
                                .then_inc(norms_clipped, 1)
                            pool.wait_ge(norms_clipped, s.count)
                            pool.tensor_tensor(inv_norm[:, n % 2], clipped[:, n % 2], exponent[:], ALU.pow)\
                                .then_inc(norms_ready, 1)
                        if s.kind == "rope_cos":
                            pool.wait_ge(by_cos_done, s.count)
                            pool.wait_ge(by_sin_done, 2 * s.count)
                            pool.wait_ge(norms_ready, s.count)
                            after_use(pool, turn_filled, "turn_k", n - 1)
                            for w in range(2):
                                pool.tensor_tensor(work_a[:, w], work_a[:, w], work_b[:, w], ALU.add).then_inc(rope_added, 1)
                                pool.wait_ge(rope_added, 2 * s.count - 1 + w)
                                norms = inv_norm[:, n % 2, w * H2:(w + 1) * H2].unsqueeze(2).to_broadcast([P, H2, HD2])
                                pool.tensor_tensor(rot[:, w * INNER:(w + 1) * INNER].rearrange("p (h d) -> p h d", d=HD2),
                                                   work_a[:, w], norms, ALU.mult).then_inc(rotated, 1)
                        if s.kind == "y_stats":
                            pool.wait_ge(y_mean, s.count)
                            inverse_root(mean_var[:, n % 2, 1:2], var_eps[:, n % 2], rstd[:, n % 2], y_eps, y_rstd, s.count)
                        if s.kind == "bias":
                            after(pool, y_normed, "ln_apply", n, per=2)
                            after(pool, y_normed, "ln_apply", n + 1, per=2)
                            pool.tensor_tensor(y[:, n % T, :], y[:, n % T, :], b2_all[:], ALU.add).then_inc(y_biased, 1)
                        if s.kind == "finish_mean" and last:
                            pool.wait_ge(f_mean, s.count)
                            inverse_root(f_mean_var[:, n % MGRP, 1:2], f_var_eps[:, n % MGRP], f_rstd[:, n % MGRP], f_eps, f_rstd_done,
                                         s.count)

            nc.all_engine_barrier(sems_to_clear=range(min(sem_nums), max(sem_nums) + 1))

        sem_nums = [s.num for s in sems]

        pieces = []

        def piece(src, terms_of, rows=P):
            pieces.append((src, terms_of, rows))

        for k in range(KC):
            for w, total, src in ((wqkv_t, 3 * INNER, wqkv), (w1_t, 2 * HID, w1)):
                for c in range(0, total, 2 * INNER):
                    cols = slice(c, min(c + 2 * INNER, total))
                    piece(src[layer, k * P:(k + 1) * P, cols], [w[e][:, k, cols] for e in range(2)])
        piece(wo[layer].rearrange("(k p) n -> p k n", p=P), [wo_t[e][:] for e in range(2)])
        for a, b in ((0, 3), (3, HCH - 1)):
            piece(w2[layer, a * HCW:b * HCW, :].rearrange("(k p) n -> p k n", p=HCW),
                  [w2_t[e][:, a:b, :] for e in range(2)], HCW)
        tail = HID - (HCH - 1) * HCW
        piece(w2[layer, (HCH - 1) * HCW:HID, :], [w2_t[e][0:tail, HCH - 1, :] for e in range(2)], tail)
        halves = probs.rearrange("p (e h) k -> p e (h k)", e=2)
        staging = [work_a.rearrange("p w h d -> p (w h d)"), work_b.rearrange("p w h d -> p (w h d)"),
                   halves[:, 0], halves[:, 1]]

        def staged(k):
            src, out, rows = pieces[k]
            tile = staging[k % STAGES][0:rows, 0:int(np.prod(out[0].shape[1:]))]
            return tile if len(out[0].shape) == 2 else tile.rearrange("p (a b) -> p a b", a=out[0].shape[1])

        with nc.Block() as block:
            @block.sync
            def _(sp):
                for k, (src, _, _) in enumerate(pieces):
                    if k >= STAGES:
                        sp.wait_ge(stage_lo, k + 1 - STAGES)
                    sp.dma_start(staged(k), src).then_inc(stage_loaded[k % STAGES], 16)

            constants = [
                (mask[:], mask_in), (ident[:], ident_in),
                (rope_c[:], tables[0].rearrange("(t p) w d -> p t w d", p=P)),
                (rope_s[:], tables[1].rearrange("(t p) w d -> p t w d", p=P)),
                (gain[:], ln_g[layer].rearrange("(k p) -> p k", p=P)),
                (shift[:], ln_b[layer].rearrange("(k p) -> p k", p=P)),
                (b2_all[:], b2[layer].partition_broadcast(P)),
                (scales[:, 0], q_scale[layer].partition_broadcast(P)),
                (scales[:, 1], k_scale[layer].partition_broadcast(P)),
            ]
            for half, to in enumerate((b1_a, b1_g)):
                full = (HCH - 1) * HCW
                constants.append((to[:, 0:HCH - 1], b1[layer, half * HID:half * HID + full].rearrange("(k p) -> p k", p=HCW)))
                constants.append((to[0:tail, HCH - 1:HCH],
                                  b1[layer, half * HID + full:(half + 1) * HID].rearrange("(p k) -> p k", k=1)))

            @block.scalar
            def _(act):
                for out, src in constants:
                    act.dma_start(out, src, allow_slow_non_contiguous=True).then_inc(constants_loaded, 16)
                for k, (_, out, _) in enumerate(pieces):
                    act.wait_ge(stage_loaded[k % STAGES], 16 * (k // STAGES + 1))
                    act.copy(out[0], staged(k)).then_inc(stage_hi, 1)

            @block.gpsimd
            def _(pool):
                pool.memset(exponent[:], -0.5)
                pool.memset(zero_col[:], 0.0)
                pool.memset(zero_row[:], 0.0)

            @block.vector
            def _(dve):
                for k, (_, out, _) in enumerate(pieces):
                    dve.wait_ge(stage_hi, k + 1)
                    dve.tensor_tensor(out[1], staged(k), out[0].bitcast(F32), ALU.subtract).then_inc(stage_lo, 1)
                dve.wait_ge(constants_loaded, 16 * len(constants))
                for w in range(2):
                    dve.tensor_tensor(rope_c[:, :, w], rope_c[:, :, w],
                                      scales[:, w].unsqueeze(1).to_broadcast([P, T, HD2]), ALU.mult)
                    for e in range(2):
                        to, of = slice(32 * e, 32 * e + 32), slice(32 - 32 * e, 64 - 32 * e)
                        dve.tensor_tensor(rope_s[:, :, w, to], rope_s[:, :, w, to],
                                          scales[:, w, of].unsqueeze(1).to_broadcast([P, T, HD2 // 2]), ALU.mult)
        nc.all_engine_barrier(sems_to_clear=range(min(sem_nums), max(sem_nums) + 1))
        section("first", 0)
        with nc.Fori(1, B * T // BODY) as i:
            section("body", i)
        section("last", B * T // BODY)


def rope_tables():
    exponents = -np.arange(0, HD1, 2).astype(np.float32) / np.float32(HD1)
    angles = np.arange(S, dtype=np.float32)[:, None] * (np.float32(10000.0) ** exponents)[None, :]
    cos, sin = np.cos(angles), np.sin(angles)
    return np.repeat(cos, 2, axis=1), np.stack([-sin, sin], -1).reshape(S, HD1)


def xpos_tables():
    f32 = np.float32
    half = np.arange(0, HD2, 2, dtype=f32)
    t = np.arange(S, dtype=f32)
    angles = t[:, None] * (f32(1.0) / f32(10000.0) ** (half / f32(HD2)))[None, :]
    scale = ((half + f32(0.4 * HD2)) / f32(1.4 * HD2))[None, :] ** ((t - S // 2) / f32(WINDOW // 2))[:, None]
    cos, sin = np.cos(angles), np.sin(angles)
    cos, scale = np.concatenate([cos, cos], -1), np.concatenate([scale, scale], -1)
    sin = np.concatenate([-sin, sin], -1)
    grow, fall = scale * f32(-QK_SCALE), f32(1.0) / scale
    return (np.stack([cos * grow, cos * fall], 1).astype(f32), np.stack([sin * grow, sin * fall], 1).astype(f32))


def window_mask():
    i, j = np.arange(P)[:, None], np.arange(2 * WINDOW)[None, :]
    outside = np.where((j < i) | (j > i + WINDOW), np.float32(MASKED), np.float32(0.0))
    return np.repeat(outside[:, None, :], 2, axis=1)


LAYER_INS = ("wqkv", "q_scale", "k_scale", "wo", "ln_g", "ln_b", "w1", "b1", "w2", "b2")


def kernel(**inputs):
    import concourse.bacc as bacc
    from concourse.bass_utils import run_bass_kernel_spmd

    nc = bacc.Bacc("TRN2", target_bir_lowering=False, num_devices=1)
    arrays = {}

    def given(name, a):
        arrays[name] = np.ascontiguousarray(a)
        return nc.dram_tensor(name, arrays[name].shape, mybir.dt.from_np(arrays[name].dtype), kind="ExternalInput").ap()

    first = {k: inputs["L0_attn_" + k] for k in ("x", "Wq", "bq", "Wk", "bk", "Wv", "bv", "Wo")}
    cos, sin = rope_tables()
    xpos_cos, xpos_sin = xpos_tables()
    ident = given("ident", np.eye(P, dtype=np.float32))
    x1 = nc.dram_tensor("x1_scratch", (B + 1, S, D), F32, kind="Internal").ap()
    x2 = nc.dram_tensor("x2_scratch", (B, S, D), F32, kind="Internal").ap()
    out = nc.dram_tensor("out", (B, S, D), F32, kind="ExternalOutput").ap()

    attention_pass(nc, given("x", first["x"]),
                   given("wqkv_t", np.concatenate([first["Wq"], first["Wk"], first["Wv"]]).T),
                   given("bqkv", np.concatenate([first["bq"], first["bk"], first["bv"]])),
                   given("wo_t", np.asarray(first["Wo"]).T),
                   given("rope_cos", cos), given("rope_sin", sin), ident, x1)
    weights = [given("layers_" + name, inputs["L0_ffn_" + name]) for name in LAYER_INS]
    tables = given("xpos_cos", xpos_cos), given("xpos_sin", xpos_sin)
    mask = given("window_mask", window_mask())
    layer_pass(nc, 0, False, x1[1:], None, x2, *weights, tables, mask, ident)
    layer_pass(nc, 1, True, x2, x1[1:], out, *weights, tables, mask, ident)

    result = run_bass_kernel_spmd(nc, [arrays], core_ids=[0])
    return result.results[0]["out"]
```
